# Optimizing a Trainium2 kernel written in Bass

```python
import numpy as np
import jax
import jax.numpy as jnp

def _softmax(x, axis=-1):
    return jax.nn.softmax(x, axis=axis)

def _gelu(x):
    return jax.nn.gelu(x, approximate=True)

def _silu(x):
    return jax.nn.silu(x)

def _sigmoid(x):
    return jax.nn.sigmoid(x)

def _layernorm(x, axis=-1, eps=1e-05):
    m = jnp.mean(x, axis=axis, keepdims=True)
    v = jnp.var(x, axis=axis, keepdims=True)
    return (x - m) / jnp.sqrt(v + eps)

def _scatter_add(tgt, idx, src, axis=0):
    return tgt.at[idx].add(src)

def _segment_sum(src, seg, n):
    return jax.ops.segment_sum(src, seg, n)
kernel_name = 'mk_sandwich_d1_jaxref_r8_0ef9d7'

def setup_inputs(seed: int=0):
    np.random.seed(seed)
    _w = jnp.asarray

    def _L0_attn_setup():
        import jax, jax.numpy as jnp
        import numpy as np
        D_MODEL = 128
        Q_HEADS = 16
        KV_HEADS = 4
        HEAD_DIM = D_MODEL // Q_HEADS
        KV_DIM = HEAD_DIM * KV_HEADS
        GROUPS = Q_HEADS // KV_HEADS
        LN_EPS = 1e-05
        NEG_INF = -10000000000.0
        key = jax.random.key(seed)
        ks = jax.random.split(key, 6)
        b, n = (2, 256)

        def xavier(k, fan_in, fan_out):
            limit = np.sqrt(6.0 / (fan_in + fan_out)).astype(np.float32)
            return jax.random.uniform(k, (fan_in, fan_out), jnp.float32, -limit, limit)
        return {'x': jax.random.normal(ks[0], (b, n, D_MODEL), jnp.float32), 'Wq': xavier(ks[1], D_MODEL, D_MODEL), 'bq': jnp.zeros((D_MODEL,), jnp.float32), 'Wk': xavier(ks[2], D_MODEL, KV_DIM), 'bk': jnp.zeros((KV_DIM,), jnp.float32), 'Wv': xavier(ks[3], D_MODEL, KV_DIM), 'bv': jnp.zeros((KV_DIM,), jnp.float32), 'ln_g': jnp.ones((D_MODEL,), jnp.float32), 'ln_b': jnp.zeros((D_MODEL,), jnp.float32), 'Wo': xavier(ks[4], D_MODEL, D_MODEL), 'bo': jnp.zeros((D_MODEL,), jnp.float32)}
    _L0_attn_in = _L0_attn_setup()

    def _L0_ffn_setup():
        import jax, jax.numpy as jnp
        import numpy as np
        D_MODEL = 128
        NHEAD = 16
        HEAD_DIM = D_MODEL // NHEAD
        FF = 256
        NUM_EXPERTS = 8
        EPS = 1e-05

        def _ln(x, g, b):
            m = x.mean(-1, keepdims=True)
            v = ((x - m) ** 2).mean(-1, keepdims=True)
            return (x - m) / jnp.sqrt(v + EPS) * g + b

        def _attention(src, Wq, bq, Wk, bk, Wv, bv, Wo, bo):
            B, T, d = src.shape
            scale = HEAD_DIM ** (-0.5)
            q = (src @ Wq + bq).reshape(B, T, NHEAD, HEAD_DIM)
            k = (src @ Wk + bk).reshape(B, T, NHEAD, HEAD_DIM)
            v = (src @ Wv + bv).reshape(B, T, NHEAD, HEAD_DIM)
            scores = jnp.einsum('bqhd,bkhd->bhqk', q, k) * scale
            probs = jax.nn.softmax(scores, axis=-1)
            out = jnp.einsum('bhqk,bkhd->bqhd', probs, v).reshape(B, T, d)
            return out @ Wo + bo

        def _moe(x, gW, gb, W1, b1, W2, b2):
            B, T, d = x.shape
            xf = x.reshape(-1, d)
            gates = jax.nn.softmax(xf @ gW + gb, axis=-1)
            top2_scores, top2_idx = jax.lax.top_k(gates, 2)
            w = (jax.nn.one_hot(top2_idx, NUM_EXPERTS, dtype=xf.dtype) * top2_scores[..., None]).sum(1)
            h = jax.nn.relu(jnp.einsum('nd,edf->enf', xf, W1) + b1[:, None, :])
            y = jnp.einsum('enf,efd->end', h, W2) + b2[:, None, :]
            out = jnp.einsum('ne,end->nd', w, y)
            return out.reshape(B, T, d)
        key = jax.random.key(seed)
        ks = jax.random.split(key, 12)
        s = 0.02
        d, f, E = (D_MODEL, FF, NUM_EXPERTS)
        return {'src': jax.random.normal(ks[0], (8, 64, d), dtype=jnp.float32), 'Wq': jax.random.normal(ks[1], (d, d), dtype=jnp.float32) * s, 'bq': jnp.zeros((d,), jnp.float32), 'Wk': jax.random.normal(ks[2], (d, d), dtype=jnp.float32) * s, 'bk': jnp.zeros((d,), jnp.float32), 'Wv': jax.random.normal(ks[3], (d, d), dtype=jnp.float32) * s, 'bv': jnp.zeros((d,), jnp.float32), 'Wo': jax.random.normal(ks[4], (d, d), dtype=jnp.float32) * s, 'bo': jnp.zeros((d,), jnp.float32), 'gW': jax.random.normal(ks[5], (d, E), dtype=jnp.float32) * s, 'gb': jnp.zeros((E,), jnp.float32), 'W1': jax.random.normal(ks[6], (E, d, f), dtype=jnp.float32) * s, 'b1': jnp.zeros((E, f), jnp.float32), 'W2': jax.random.normal(ks[7], (E, f, d), dtype=jnp.float32) * s, 'b2': jnp.zeros((E, d), jnp.float32), 'ln1_g': jnp.ones((d,), jnp.float32), 'ln1_b': jnp.zeros((d,), jnp.float32), 'ln2_g': jnp.ones((d,), jnp.float32), 'ln2_b': jnp.zeros((d,), jnp.float32)}
    _L0_ffn_in = _L0_ffn_setup()
    _d = {'L0_attn_x': _L0_attn_in['x'], 'L0_attn_Wq': _L0_attn_in['Wq'], 'L0_attn_bq': _L0_attn_in['bq'], 'L0_attn_Wk': _L0_attn_in['Wk'], 'L0_attn_bk': _L0_attn_in['bk'], 'L0_attn_Wv': _L0_attn_in['Wv'], 'L0_attn_bv': _L0_attn_in['bv'], 'L0_attn_ln_g': _L0_attn_in['ln_g'], 'L0_attn_ln_b': _L0_attn_in['ln_b'], 'L0_attn_Wo': _L0_attn_in['Wo'], 'L0_attn_bo': _L0_attn_in['bo'], 'L0_ffn_Wq': _L0_ffn_in['Wq'], 'L0_ffn_bq': _L0_ffn_in['bq'], 'L0_ffn_Wk': _L0_ffn_in['Wk'], 'L0_ffn_bk': _L0_ffn_in['bk'], 'L0_ffn_Wv': _L0_ffn_in['Wv'], 'L0_ffn_bv': _L0_ffn_in['bv'], 'L0_ffn_Wo': _L0_ffn_in['Wo'], 'L0_ffn_bo': _L0_ffn_in['bo'], 'L0_ffn_gW': _L0_ffn_in['gW'], 'L0_ffn_gb': _L0_ffn_in['gb'], 'L0_ffn_W1': _L0_ffn_in['W1'], 'L0_ffn_b1': _L0_ffn_in['b1'], 'L0_ffn_W2': _L0_ffn_in['W2'], 'L0_ffn_b2': _L0_ffn_in['b2'], 'L0_ffn_ln1_g': _L0_ffn_in['ln1_g'], 'L0_ffn_ln1_b': _L0_ffn_in['ln1_b'], 'L0_ffn_ln2_g': _L0_ffn_in['ln2_g'], 'L0_ffn_ln2_b': _L0_ffn_in['ln2_b']}
    _x0 = _d['L0_attn_x']
    _d['L0_attn_x'] = jax.random.normal(jax.random.fold_in(jax.random.key(seed), 1), (4, 1024, 128), dtype=_x0.dtype)
    del _x0
    return _d

def reference(L0_attn_x, L0_attn_Wq, L0_attn_bq, L0_attn_Wk, L0_attn_bk, L0_attn_Wv, L0_attn_bv, L0_attn_ln_g, L0_attn_ln_b, L0_attn_Wo, L0_attn_bo, L0_ffn_Wq, L0_ffn_bq, L0_ffn_Wk, L0_ffn_bk, L0_ffn_Wv, L0_ffn_bv, L0_ffn_Wo, L0_ffn_bo, L0_ffn_gW, L0_ffn_gb, L0_ffn_W1, L0_ffn_b1, L0_ffn_W2, L0_ffn_b2, L0_ffn_ln1_g, L0_ffn_ln1_b, L0_ffn_ln2_g, L0_ffn_ln2_b):

    def _L0_attn_ref(x, Wq, bq, Wk, bk, Wv, bv, ln_g, ln_b, Wo, bo):
        import jax, jax.numpy as jnp
        import numpy as np
        D_MODEL = 128
        Q_HEADS = 16
        KV_HEADS = 4
        HEAD_DIM = D_MODEL // Q_HEADS
        KV_DIM = HEAD_DIM * KV_HEADS
        GROUPS = Q_HEADS // KV_HEADS
        LN_EPS = 1e-05
        NEG_INF = -10000000000.0
        b, n, _ = x.shape
        q = x @ Wq + bq
        k = x @ Wk + bk
        v = x @ Wv + bv
        q = q.reshape(b, n, GROUPS, KV_HEADS, HEAD_DIM)
        q = jnp.transpose(q, (0, 2, 3, 1, 4))
        k = k.reshape(b, n, KV_HEADS, HEAD_DIM)
        v = v.reshape(b, n, KV_HEADS, HEAD_DIM)
        scale = jnp.asarray(HEAD_DIM ** 0.5, q.dtype)
        q = q / scale
        attn_logits = jnp.einsum('bghnd,bmhd->bghnm', q, k)
        causal = jnp.tril(jnp.ones((n, n), dtype=bool))
        attn_logits = jnp.where(causal[None, None, None, :, :], attn_logits, NEG_INF)
        attn = jax.nn.softmax(attn_logits, axis=-1)
        out = jnp.einsum('bghnm,bmhd->bghnd', attn, v)
        out = jnp.transpose(out, (0, 3, 1, 2, 4)).reshape(b, n, D_MODEL)
        mu = jnp.mean(out, axis=-1, keepdims=True)
        var = jnp.var(out, axis=-1, keepdims=True)
        out = (out - mu) * jax.lax.rsqrt(var + LN_EPS) * ln_g + ln_b
        out = out @ Wo + bo
        return out

    def _L0_ffn_ref(src, Wq, bq, Wk, bk, Wv, bv, Wo, bo, gW, gb, W1, b1, W2, b2, ln1_g, ln1_b, ln2_g, ln2_b):
        import jax, jax.numpy as jnp
        import numpy as np
        D_MODEL = 128
        NHEAD = 16
        HEAD_DIM = D_MODEL // NHEAD
        FF = 256
        NUM_EXPERTS = 8
        EPS = 1e-05

        def _ln(x, g, b):
            m = x.mean(-1, keepdims=True)
            v = ((x - m) ** 2).mean(-1, keepdims=True)
            return (x - m) / jnp.sqrt(v + EPS) * g + b

        def _attention(src, Wq, bq, Wk, bk, Wv, bv, Wo, bo):
            B, T, d = src.shape
            scale = HEAD_DIM ** (-0.5)
            q = (src @ Wq + bq).reshape(B, T, NHEAD, HEAD_DIM)
            k = (src @ Wk + bk).reshape(B, T, NHEAD, HEAD_DIM)
            v = (src @ Wv + bv).reshape(B, T, NHEAD, HEAD_DIM)
            scores = jnp.einsum('bqhd,bkhd->bhqk', q, k) * scale
            probs = jax.nn.softmax(scores, axis=-1)
            out = jnp.einsum('bhqk,bkhd->bqhd', probs, v).reshape(B, T, d)
            return out @ Wo + bo

        def _moe(x, gW, gb, W1, b1, W2, b2):
            B, T, d = x.shape
            xf = x.reshape(-1, d)
            gates = jax.nn.softmax(xf @ gW + gb, axis=-1)
            top2_scores, top2_idx = jax.lax.top_k(gates, 2)
            w = (jax.nn.one_hot(top2_idx, NUM_EXPERTS, dtype=xf.dtype) * top2_scores[..., None]).sum(1)
            h = jax.nn.relu(jnp.einsum('nd,edf->enf', xf, W1) + b1[:, None, :])
            y = jnp.einsum('enf,efd->end', h, W2) + b2[:, None, :]
            out = jnp.einsum('ne,end->nd', w, y)
            return out.reshape(B, T, d)
        attn_out = _attention(src, Wq, bq, Wk, bk, Wv, bv, Wo, bo)
        x = _ln(src + attn_out, ln1_g, ln1_b)
        ff = _moe(x, gW, gb, W1, b1, W2, b2)
        return _ln(x + ff, ln2_g, ln2_b)
    x = L0_attn_x
    x = x + _layernorm(_L0_attn_ref(_layernorm(x, axis=-1), L0_attn_Wq, L0_attn_bq, L0_attn_Wk, L0_attn_bk, L0_attn_Wv, L0_attn_bv, L0_attn_ln_g, L0_attn_ln_b, L0_attn_Wo, L0_attn_bo), axis=-1)
    x = x + _layernorm(_L0_ffn_ref(_layernorm(x, axis=-1), L0_ffn_Wq, L0_ffn_bq, L0_ffn_Wk, L0_ffn_bk, L0_ffn_Wv, L0_ffn_bv, L0_ffn_Wo, L0_ffn_bo, L0_ffn_gW, L0_ffn_gb, L0_ffn_W1, L0_ffn_b1, L0_ffn_W2, L0_ffn_b2, L0_ffn_ln1_g, L0_ffn_ln1_b, L0_ffn_ln2_g, L0_ffn_ln2_b), axis=-1)
    return x

_drawn_inputs = setup_inputs


def setup_inputs(seed=0):
    import zlib

    import numpy as np

    out = dict(_drawn_inputs(seed))
    spreads = {'L0_attn_bq': (0.0, 0.1),
     'L0_attn_bk': (0.0, 0.8),
     'L0_attn_bv': (0.0, 0.1),
     'L0_attn_ln_g': (1.0, 0.2),
     'L0_attn_ln_b': (0.0, 0.1),
     'L0_attn_bo': (0.0, 0.1),
     'L0_ffn_bq': (0.0, 0.8),
     'L0_ffn_bk': (0.0, 0.8),
     'L0_ffn_bv': (0.0, 0.8),
     'L0_ffn_bo': (0.0, 0.1),
     'L0_ffn_gb': (0.0, 0.8),
     'L0_ffn_b1': (0.0, 0.8),
     'L0_ffn_b2': (0.0, 0.8),
     'L0_ffn_ln1_g': (1.0, 0.2),
     'L0_ffn_ln1_b': (0.0, 0.1),
     'L0_ffn_ln2_g': (1.0, 0.2),
     'L0_ffn_ln2_b': (0.0, 0.1)}
    factors = {'L0_ffn_Wq': 8.0,
     'L0_ffn_Wk': 8.0,
     'L0_ffn_Wv': 6.372,
     'L0_ffn_Wo': 4.284,
     'L0_ffn_gW': 6.537,
     'L0_ffn_W1': 8.0,
     'L0_ffn_W2': 8.0}
    for name, (base, spread) in spreads.items():
        noise = np.random.default_rng([zlib.crc32(name.encode()), seed]).standard_normal(out[name].shape)
        drawn = base * np.exp(spread * noise) if base else spread * noise
        out[name] = jnp.asarray(drawn.astype(out[name].dtype))
    for name, factor in factors.items():
        out[name] = (out[name] * factor).astype(out[name].dtype)
    return out
```

```python
import concourse.bass as bass
from concourse import mybir
from contextlib import ExitStack

FP32 = mybir.dt.float32
BF16 = mybir.dt.bfloat16
ALU = mybir.AluOpType
ACT = mybir.ActivationFunctionType
AX = mybir.AxisListType

B, N, D = 4, 1024, 128
P = 128
H, HD = 16, 8
KVH = 4
E, FF = 8, 256
NT = N // P
HG = 4
UNITS = B * H // HG
UPB = H // HG
CH = 512
NC = N // CH
QPARTS = [0, 0, 0, 1, 1, 2]
KPARTS = [0, 1, 2, 0, 1, 0]
NB = len(QPARTS)
ROWS = NB * HD
MROWS = 3
VW = HG * (HD + 1)
VPAD = 60
SCALE = float(HD) ** -0.5
EPS = 1e-5
NEG = -1e30
LEAD = 4
RING = 3
TSLOT = 4


def wait(eng, sem, value):
    if isinstance(value, int) and value <= 0:
        return
    eng.wait_ge(sem, value)


class Plan:

    def __init__(self, causal):
        self.causal = causal
        self.steps = [(c, kt) for c in range(NC) for kt in range(NT)
                      if not causal or kt * P < (c + 1) * CH]
        self.n = len(self.steps)
        self.rows = []
        for qt in range(NT):
            for half in range(NC):
                width = min(CH, (qt + 1) * P - half * CH) if causal else CH
                if width > 0:
                    self.rows += [(qt, half, width, g, r) for g in range(2) for r in range(2)]
        self.nr = len(self.rows)
        self.per = self.nr // self.n
        assert self.per == 4 and self.nr == 4 * self.n
        self.used_slots = self.nr + 1
        self.slots = -(-self.used_slots // RING) * RING

    def off(self, c, kt):
        return max(0, kt * P - c * CH) if self.causal else 0

    def first(self, c, kt):
        return kt == 0

    def last(self, s):
        return s == self.n - 1 or self.steps[s + 1][0] != self.steps[s][0]

    def slot_of(self, r):
        return r if r < TSLOT else r + 1

    def used(self, v, x):
        if isinstance(v, int) and v == 0 and x < TSLOT:
            return x + 1
        if isinstance(v, int) and v == UNITS:
            return v * self.used_slots
        return v * self.used_slots + x

    def before(self, v, x):
        alone = isinstance(v, int) and v == UNITS
        if x >= RING and not alone:
            return self.used(v, x - RING)
        y = self.slots - RING + x % RING
        while y > self.nr:
            y -= RING
        if isinstance(v, int) and v == 0:
            return 0
        return self.used(v - 1, y)

    def stream(self, u, s):
        t = s + LEAD
        v, base = (u + 1, 4 * t) if t < self.n else (u + 2, 4 * (t - self.n))
        over = isinstance(v, int) and v >= UNITS
        out = []
        for r in range(base, base + 4):
            if r == TSLOT and (not isinstance(v, int) or v <= UNITS):
                out.append((v - 1, None))
            if not over:
                out.append((v, r))
        return out


def sandwich(nc, x_d, wq1, bq1, wk1, bk1, wv1, bv1, lng1, lnb1, wo1, bo1,
             wq2, bq2, wk2, bk2, wv2, bv2, wo2, bo2, gw, gb, w1, b1, w2, b2,
             l1g, l1b, l2g, l2b, out_d):
    ctx = ExitStack()

    def sb(name, shape, dt=FP32):
        return ctx.enter_context(nc.sbuf_tensor(name, shape, dt))

    def dram(name, shape, dt):
        return nc.dram_tensor(name, shape, dt, kind="Internal").ap()

    def sem(name):
        return ctx.enter_context(nc.semaphore(name))

    with ctx:
        q_st = [dram(f"q_st{a}", (UNITS, HG, NB, HD, N), BF16) for a in range(2)]
        k_st = [dram(f"k_st{a}", (UNITS, HG, NB, HD, N), BF16) for a in range(2)]
        v_st = [dram(f"v_st{a}", (UNITS, N, VW), FP32) for a in range(2)]
        o_st = [dram(f"o_st{a}", (UNITS, HG, HD + 1, N), FP32) for a in range(2)]

        wq_s = [sb(f"wq{a}", [P, D]) for a in range(2)]
        wk_s = [sb(f"wk{a}", [P, D]) for a in range(2)]
        wv_s = [sb(f"wv{a}", [P, D]) for a in range(2)]
        wo_s = [sb(f"wo{a}", [P, D]) for a in range(2)]
        bq_s = [sb(f"bq{a}", [P, 1]) for a in range(2)]
        bk_s = [sb(f"bk{a}", [P, 1]) for a in range(2)]
        bv_s = [sb(f"bv{a}", [P, D]) for a in range(2)]
        bo_s = [sb(f"bo{a}", [P, D]) for a in range(2)]
        lng_s, lnb_s = sb("lng", [P, 1]), sb("lnb", [P, 1])
        gw_s, gb_s = sb("gw", [P, E]), sb("gb", [P, E])
        w1_s, b1_s = sb("w1", [P, E, FF]), sb("b1", [P, E, 2])
        w2_s, b2_s = sb("w2", [P, E, 2, D]), sb("b2", [E, D])
        l1g_s, l1b_s = sb("l1g", [P, D]), sb("l1b", [P, D])
        l2g_s, l2b_s = sb("l2g", [P, D]), sb("l2b", [P, D])
        ident = sb("ident", [P, P])
        identb = sb("identb", [P, P], BF16)
        mask_q = sb("mask_q", [P, P], BF16)
        mask_k = sb("mask_k", [P, P], BF16)
        before_e = sb("before_e", [P, E, E])

        X = sb("X", [P, B, NT * D])
        XH = sb("XH", [P, B, NT * D])
        xT = sb("xT", [P, N])
        nat = sb("nat", [P, NT * D])
        nat2 = sb("nat2", [P, NT * D])
        bnst = sb("bnst", [P, NT, 6])
        mean, dif = sb("mean", [P, NT]), sb("dif", [P, NT])
        std = sb("std", [P, NT])
        rstd = sb("rstd", [P, NT])
        qf = [sb("qf", [P, N]), sb("kf", [P, N])]
        parts = [[sb(f"part{t}{j}", [P, N], BF16) for j in range(3)] for t in range(2)]
        vsb = sb("vsb", [P, NT, H, HD + 1])
        oT, lB, oN = sb("oT", [P, N]), sb("lB", [P, N]), sb("oN", [P, N])
        res = sb("res", [P, NT * D])
        QS = [sb(f"QS{p}", [P, 2, N], BF16) for p in range(2)]
        KS = [[sb(f"KS{p}{h}", [P, 2, N], BF16) for h in range(2)] for p in range(2)]
        QR = [[sb(f"QR{p}{h}", [P, 2, N], BF16) for h in range(2)] for p in range(2)]
        KR = [sb(f"KR{p}", [P, 2, N], BF16) for p in range(2)]
        VS = [sb(f"VS{p}", [P, NT, VPAD]) for p in range(2)]
        PR = [sb(f"PR{p}", [P, HG, CH]) for p in range(2)]
        OS = [sb(f"OS{c}", [P, CH]) for c in range(NC)]
        mx = [sb(f"mx{p}", [P, NT, 4, 2]) for p in range(2)]
        nm, nm2 = sb("nm", [P, NT * 4]), sb("nm2", [P, NT * 4])
        mparts = [sb(f"mparts{p}", [P, NT, 2, MROWS, 2], BF16) for p in range(2)]
        mrow = [sb(f"mrow{p}", [4 * MROWS, N], BF16) for p in range(2)]
        lg, ge, wt = sb("lg", [P, NT, E]), sb("ge", [P, NT, E]), sb("wt", [P, NT, E])
        gs = sb("gs", [P, NT])
        cmp1, cmp2 = sb("cmp1", [P, NT, E, E]), sb("cmp2", [P, NT, E, E])
        wT = sb("wT", [E, N])
        hT = [sb(f"hT{p}", [P, 2, CH]) for p in range(2)]

        PS = ctx.enter_context(nc.psum_tensor("PS", [P, 8, CH], FP32))
        TB = 0
        AC = 4
        RB = 5

        wload = sem("wload")
        const_ready = sem("const_ready")
        const_dve = sem("const_dve")
        block = ctx.enter_context(nc.Block())

        loads = []

        def ld(dst, src):
            loads.append((dst, src))

        col = lambda v: v.rearrange("(p a) -> p a", a=1)
        bc = lambda v, n: v.rearrange("(a n) -> a n", a=1).to_broadcast([P, n])
        for b in range(B):
            ld(X[:, b, :].rearrange("p (t d) -> p t d", d=D), x_d[b].rearrange("(t p) d -> p t d", p=P))
        for a, (wq, wk, wv, wo, bq, bk, bv, bo) in enumerate(
                [(wq1, wk1, wv1, wo1, bq1, bk1, bv1, bo1), (wq2, wk2, wv2, wo2, bq2, bk2, bv2, bo2)]):
            ld(wq_s[a][:, :], wq)
            kv = wk.shape[1]
            for c in range(0, D, kv):
                ld(wk_s[a][:, c:c + kv], wk)
                ld(wv_s[a][:, c:c + kv], wv)
                ld(bk_s[a][c:c + kv, :], col(bk))
                ld(bv_s[a][:, c:c + kv], bc(bv, kv))
            ld(wo_s[a][:, :], wo)
            ld(bq_s[a][:, :], col(bq))
            ld(bo_s[a][:, :], bc(bo, D))
        ld(lng_s[:, :], col(lng1))
        ld(lnb_s[:, :], col(lnb1))
        ld(gw_s[:, :], gw)
        ld(gb_s[:, :], bc(gb, E))
        ld(w1_s[:, :, :], w1.rearrange("e d f -> d e f"))
        for e in range(E):
            ld(b1_s[:, e, :], b1[e].rearrange("(a f) -> f a", a=2))
        for e in range(E):
            ld(w2_s[:, e, :, :], w2[e].rearrange("(a f) d -> f a d", a=2))
        ld(b2_s[:, :], b2)
        for dst, src in ((l1g_s, l1g), (l1b_s, l1b), (l2g_s, l2g), (l2b_s, l2b)):
            ld(dst[:, :], bc(src, D))
        LOADED = 16 * len(loads)


        def signals(phase, names):
            return {name: sem(f"{phase}_{name}") for name in names.split()}

        PREP = ("chain var_ready std_ready xh_ready xt_psum xt_ready q_psum k_psum v_psum qk_taken "
                "xh_kept q_parts k_ready k_parts v_ready qst_stored kst_stored vst_stored k_rounded k_rest")
        prep = [signals(f"prep{a}", PREP) for a in range(2)]
        MID = ("chain o_loaded l_loaded on_ready on_psum var_ready std_ready ln_ready ln_psum "
               "lnt_ready y_psum on_free x_ready")
        mid = signals("mid", MID)
        TAIL = ("chain o_loaded l_loaded on_ready on_free y_psum var_ready std_ready xf_ready xf_psum "
                "xt_ready logit_psum shifted exp_ready wt_ready wt_psum wT_ready bias_psum acc_ready "
                "h_psum h_ready e_psum e_added out_ready out_stored")
        tail = signals("tail", TAIL)
        ATT = ("row_ready row_read chain max_ready maxrow_ready scores_a scores_b exp_a exp_b pv_done "
               "acc_copied")
        att = [signals(f"att{a}", ATT) for a in range(2)]
        for a in range(2):
            for name, n in (("row_loaded", 2), ("main_loaded", 2), ("maxrow_loaded", 2), ("o_stored", NC)):
                att[a][name] = [sem(f"att{a}_{name}{p}") for p in range(n)]
        plans = [Plan(True), Plan(False)]

        class Chain:

            def __init__(self, eng, counts, base):
                self.eng, self.counts, self.base, self.n = eng, counts, base, 0

            def link(self, ins):
                self.n += 1
                ins.then_inc(self.counts, 1)
                self.eng.wait_ge(self.counts, self.base + self.n)

        def norm_stats(dve, chain, src, S, at):
            for t in range(NT):
                ins = nc.vector.bn_stats(bnst[:, t, :], src(t))
            chain.link(ins)
            mean_e, sq_e, mean_o, sq_o = (bnst[:, :, k] for k in (1, 2, 4, 5))
            nc.vector.tensor_tensor(mean[:, :], mean_e, mean_o, ALU.add)
            nc.vector.tensor_tensor(dif[:, :], mean_e, mean_o, ALU.subtract)
            chain.link(nc.vector.scalar_tensor_tensor(std[:, :], sq_e, D * EPS, sq_o, ALU.add, ALU.add))
            nc.vector.tensor_scalar(mean[:, :], mean[:, :], 0.5, None, ALU.mult)
            chain.link(nc.vector.scalar_tensor_tensor(dif[:, :], dif[:, :], D / 4.0, dif[:, :],
                                                      ALU.mult, ALU.mult))
            nc.vector.tensor_tensor(std[:, :], std[:, :], dif[:, :], ALU.add).then_inc(S["var_ready"], 1)
            dve.wait_ge(S["std_ready"], at)
            chain.link(nc.vector.reciprocal(rstd[:, :], std[:, :]))

        def root(act, S, at):
            act.wait_ge(S["var_ready"], at)
            nc.scalar.activation(std[:, :], std[:, :], ACT.Sqrt, scale=1.0 / D).then_inc(S["std_ready"], 1)

        def normalise(dst, src):
            for t in range(NT):
                ins = nc.vector.tensor_scalar(dst[:, t * D:(t + 1) * D], src(t),
                                              mean[:, t:t + 1], rstd[:, t:t + 1], ALU.subtract, ALU.mult)
            return ins

        def tile(buf):
            return lambda t: buf[:, t * D:(t + 1) * D]

        def psum_tile(bank):
            return lambda t: PS[:, bank + t // 4, (t % 4) * D:(t % 4 + 1) * D]

        def wide(v):
            return v[:, :].rearrange("p (a d) -> p a d", a=1).to_broadcast([P, NT, D])

        def banks(bank):
            return PS[:, bank:bank + 2, :].rearrange("p c (t d) -> p (c t) d", d=D)

        def tiles(buf):
            return buf[:, :].rearrange("p (t d) -> p t d", d=D)

        def spread(x):
            return x.rearrange("p (t d) -> p t d", d=D)

        PREP_CHAIN = 8

        def prep_dve(dve, a):
            S = prep[a]
            with dve.Fori(0, B) as b:
                ch = Chain(dve, S["chain"], b * PREP_CHAIN)
                norm_stats(dve, ch, tile(X[:, b, :]), S, b + 1)
                normalise(nat, tile(X[:, b, :])).then_inc(S["xh_ready"], 1)
                dve.wait_ge(S["q_psum"], b + 1)
                dve.wait_ge(S["qst_stored"], b * (16 * NB) + 1)
                ch.link(nc.vector.tensor_scalar(qf[0][:, :], PS[:, 2:4, :], bq_s[a][:, :], SCALE,
                                                ALU.add, ALU.mult))
                dve.wait_ge(S["k_psum"], b + 1)
                dve.wait_ge(S["k_parts"], b + 1)
                nc.vector.tensor_scalar(qf[1][:, :], PS[:, 4:6, :], bk_s[a][:, :], None,
                                        ALU.add).then_inc(S["k_ready"], 1)
                q, (q0, q1, q2) = qf[0][:, :], [x[:, :] for x in parts[0]]
                ch.link(nc.vector.tensor_copy(q0, q))
                ch.link(nc.vector.tensor_tensor(q, q, q0, ALU.subtract))
                ch.link(nc.vector.tensor_copy(q1, q))
                nc.vector.tensor_tensor(q2, q, q1, ALU.subtract).then_inc(S["q_parts"], 1)
                dve.wait_ge(S["v_psum"], b + 1)
                dve.wait_ge(S["vst_stored"], b * (16 * UPB) + 1)
                for c in range(2):
                    ins = nc.vector.tensor_tensor(
                        vsb[:, 4 * c:4 * c + 4, :, 0:HD],
                        PS[:, 6 + c, :].rearrange("p (t h d) -> p t h d", t=4, d=HD),
                        bv_s[a][:, :].rearrange("p (a h d) -> p a h d", a=1, d=HD).to_broadcast([P, 4, H, HD]),
                        ALU.add)
                ins.then_inc(S["v_ready"], 1)
                assert ch.n == PREP_CHAIN, ch.n

        def prep_act(act, a):
            S = prep[a]
            with act.Fori(0, B) as b:
                root(act, S, b + 1)
                if a == 1:
                    act.wait_ge(S["xh_ready"], b + 1)
                    nc.scalar.copy(XH[:, b, :], nat[:, :]).then_inc(S["xh_kept"], 1)
                for c in range(2):
                    act.wait_ge(S["xt_psum"], 2 * b + c + 1)
                    nc.scalar.copy(xT[:, c * CH:(c + 1) * CH], PS[:, c, :]).then_inc(S["xt_ready"], 1)
                act.wait_ge(S["k_ready"], b + 1)
                act.wait_ge(S["kst_stored"], b * (16 * NB) + 1)
                nc.scalar.copy(parts[1][0][:, :], qf[1][:, :]).then_inc(S["k_rounded"], 1)
                act.wait_ge(S["k_rest"], b + 1)
                nc.scalar.copy(parts[1][1][:, :], qf[1][:, :]).then_inc(S["k_rounded"], 1)

        def prep_pe(pe, a):
            S = prep[a]
            with pe.Fori(0, B) as b:
                pe.wait_ge(S["xh_ready"], b + 1)
                for t in range(NT):
                    ins = nc.tensor.transpose(PS[:, t // 4, (t % 4) * P:(t % 4 + 1) * P],
                                              nat[:, t * D:(t + 1) * D], ident[:, :])
                    if t % 4 == 3:
                        ins.then_inc(S["xt_psum"], 1)
                pe.wait_ge(S["xt_ready"], 2 * b + 2)
                for bank, w, signal in ((2, wq_s[a], S["q_psum"]), (4, wk_s[a], S["k_psum"])):
                    for c in range(2):
                        ins = nc.tensor.matmul(PS[:, bank + c, :], w[:, :], xT[:, c * CH:(c + 1) * CH],
                                               start=True, stop=True)
                    ins.then_inc(signal, 1)
                for t in range(NT):
                    ins = nc.tensor.matmul(PS[:, 6 + t // 4, (t % 4) * D:(t % 4 + 1) * D],
                                           xT[:, t * P:(t + 1) * P], wv_s[a][:, :], start=True, stop=True)
                ins.then_inc(S["v_psum"], 1)

        def prep_pool(pool, a):
            S = prep[a]
            pool.sem_inc(S["k_parts"], 1)
            with pool.Fori(0, B) as b:
                k, (k0, k1, k2) = qf[1][:, :], [x[:, :] for x in parts[1]]
                pool.wait_ge(S["k_rounded"], 2 * b + 1)
                nc.gpsimd.tensor_tensor(k, k, k0, ALU.subtract).then_inc(S["k_rest"], 1)
                pool.wait_ge(S["k_rounded"], 2 * b + 2)
                nc.gpsimd.tensor_tensor(k2, k, k1, ALU.subtract).then_inc(S["k_parts"], 1)

        def prep_sp(sp, a):
            S = prep[a]
            for signal in (S["qst_stored"], S["kst_stored"], S["vst_stored"]):
                sp.sem_inc(signal, 1)
            with sp.Fori(0, B) as b:
                for st, which, pt, signal, ready, more in (
                        (q_st[a], QPARTS, parts[0], S["qst_stored"], S["q_parts"], 1),
                        (k_st[a], KPARTS, parts[1], S["kst_stored"], S["k_parts"], 2)):
                    sp.wait_ge(ready, b + more)
                    view = st.rearrange("(b u) j c d n -> b c (u j) d n", u=UPB)[b]
                    for c in range(NB):
                        sp.dma_start(view[c], pt[which[c]][:, :]).then_inc(signal, 16)
                sp.wait_ge(S["v_ready"], b + 1)
                view = v_st[a].rearrange("(b u) (t p) w -> b u p t w", u=UPB, p=P)[b]
                for u in range(UPB):
                    sp.dma_start(view[u], vsb[:, :, HG * u:HG * u + HG, :].rearrange("p t h d -> p t (h d)")
                                 ).then_inc(S["vst_stored"], 16)
            sp.wait_ge(S["qst_stored"], 1 + B * 16 * NB)
            sp.wait_ge(S["kst_stored"], 1 + B * 16 * NB)
            sp.wait_ge(S["vst_stored"], 1 + B * 16 * UPB)

        CHAIN = 4

        def pairwise(eng, body):
            for i in (0,):
                for p in range(2):
                    body(2 * i + p, p, i)
            with eng.Fori(1, UNITS // 2 - 1) as i:
                for p in range(2):
                    body(2 * i + p, p, i)
            for i in (UNITS // 2 - 1,):
                for p in range(2):
                    body(2 * i + p, p, i)

        def ahead(v, p, i, d):
            return v + d, (p + d) % 2, i + (p + d) // 2

        def att_pe(pe, a):
            S, pl = att[a], plans[a]

            def row_scores(v, vp, vi, r):
                qt, half, width, g, hp = pl.rows[r]
                if r == 0:
                    pe.wait_ge(S["row_loaded"][vp], 64 * (vi + 1))
                x = pl.slot_of(r)
                wait(pe, S["row_read"], pl.before(v, x))
                bank = RB + x % RING
                diagonal = pl.causal and qt // 4 == half
                ins = nc.tensor.matmul(PS[:, bank, 0:width], QR[vp][hp][:, g, qt * P:(qt + 1) * P],
                                       KR[vp][:, g, half * CH:half * CH + width],
                                       start=True, stop=not diagonal)
                if diagonal:
                    ins = nc.tensor.matmul(PS[:, bank, width - P:width], identb[:, :], mask_q[:, :],
                                           start=False, stop=True)
                ins.then_inc(S["row_ready"], 1)

            def transpose_maxima(v, vp, stream):
                pe.wait_ge(S["max_ready"], v + 1)
                wait(pe, S["row_read"], pl.before(stream, TSLOT))
                bank = PS[:, RB + TSLOT % RING, :].bitcast(BF16)
                for qt in range(NT):
                    ins = nc.tensor.transpose(bank[0:4 * MROWS, qt * P:(qt + 1) * P],
                                              mparts[vp][:, qt, :, :, :].rearrange("p r m g -> p (r m g)"),
                                              identb[:, :])
                ins.then_inc(S["row_ready"], 1)

            def scores(u, p, i, s, g):
                c, kt = pl.steps[s]
                off = pl.off(c, kt)
                done, signal = (S["exp_a"], S["scores_a"]) if g == 0 else (S["exp_b"], S["scores_b"])
                if s == 0 and g == 0:
                    pe.wait_ge(S["main_loaded"][p], 80 * (i + 1))
                    pe.wait_ge(S["maxrow_loaded"][p], 16 * 2 * MROWS * (i + 1))
                wait(pe, done, pl.n * u + s)
                diagonal = pl.causal and kt // 4 == c
                for hp in range(2):
                    ins = nc.tensor.matmul(PS[:, TB + 2 * g + hp, off:CH], KS[p][hp][:, g, kt * P:(kt + 1) * P],
                                           QS[p][:, g, c * CH + off:(c + 1) * CH],
                                           start=True, stop=not diagonal)
                if diagonal:
                    for hp in range(2):
                        ins = nc.tensor.matmul(PS[:, TB + 2 * g + hp, off:off + P], identb[:, :],
                                               mask_k[:, :], start=False, stop=True)
                ins.then_inc(signal, 1)

            def values(u, p, s):
                c, kt = pl.steps[s]
                off = pl.off(c, kt)
                pe.wait_ge(S["exp_b"], pl.n * u + s + 1)
                if kt == 0:
                    wait(pe, S["acc_copied"], NC * u + c)
                for h in range(HG):
                    ins = nc.tensor.matmul(PS[32 * h:32 * h + 32, AC, off:CH],
                                           VS[p][:, kt, 9 * h:9 * h + 32], PR[s % 2][:, h, off:CH],
                                           start=kt == 0, stop=pl.last(s))
                ins.then_inc(S["pv_done"], 1)

            def body(u, p, i):
                for s in range(pl.n):
                    more = pl.stream(u, s)
                    cut = max(len(more) - 2, 0) if len(more) > 1 else 1
                    if s + 1 < pl.n:
                        nxt = (u, p, i, s + 1)
                    else:
                        nxt = (*ahead(u, p, i, 1), 0)
                    run_next = not (isinstance(nxt[0], int) and nxt[0] == UNITS)

                    def maxima(items):
                        for v, r in items:
                            if r is None:
                                transpose_maxima(v, (p + 1) % 2, v + 1)
                            else:
                                d = 1 if s + LEAD < pl.n else 2
                                _, vp, vi = ahead(u, p, i, d)
                                row_scores(v, vp, vi, r)

                    if run_next:
                        scores(*nxt, 0)
                    maxima(more[:cut])
                    if run_next:
                        scores(*nxt, 1)
                    maxima(more[cut:])
                    values(u, p, s)

            for r in range(pl.nr):
                row_scores(0, 0, 0, r)
            for r in range(TSLOT):
                row_scores(1, 1, 0, r)
            transpose_maxima(0, 0, 1)
            for r in range(TSLOT, 4 * LEAD):
                row_scores(1, 1, 0, r)
            scores(0, 0, 0, 0, 0)
            scores(0, 0, 0, 0, 1)
            pairwise(pe, body)

        def att_dve(dve, a):
            S, pl = att[a], plans[a]

            def row_max(v, vp, r):
                qt, half, width, g, hp = pl.rows[r]
                x = pl.slot_of(r)
                dve.wait_ge(S["row_ready"], pl.used(v, x))
                nc.vector.tensor_reduce(mx[vp][:, qt, 2 * hp + g, half:half + 1],
                                        PS[:, RB + x % RING, 0:width], AX.X, ALU.max,
                                        negate=True).then_inc(S["row_read"], 1)
                if r == pl.nr - 1:
                    parts_of_max(v, vp)

            def parts_of_max(v, vp):
                dve.wait_ge(S["row_read"], pl.used(v, pl.nr))
                ch = Chain(dve, S["chain"], v * CHAIN)
                m4 = mparts[vp]
                f = nm[:, :].rearrange("p (t r g) -> p t r g", r=2, g=2)
                f2 = nm2[:, :].rearrange("p (t r g) -> p t r g", r=2, g=2)
                ch.link(nc.vector.tensor_reduce(nm[:, :], mx[vp][:, :, :, :].rearrange("p t h k -> p (t h) k"),
                                                AX.X, ALU.min))
                ch.link(nc.vector.tensor_copy(m4[:, :, :, 0, :], f))
                ch.link(nc.vector.tensor_tensor(f2, f, m4[:, :, :, 0, :], ALU.subtract))
                ch.link(nc.vector.tensor_copy(m4[:, :, :, 1, :], f2))
                ins = nc.vector.tensor_tensor(m4[:, :, :, 2, :], f2, m4[:, :, :, 1, :], ALU.subtract)
                ins.then_inc(S["max_ready"], 1)
                dve.wait_ge(S["max_ready"], v + 1)
                assert ch.n == CHAIN

            def rows_of_max(v, vp, i_prev, stream):
                dve.wait_ge(S["row_ready"], pl.used(stream, TSLOT))
                if not (isinstance(v, int) and v < 2):
                    dve.wait_ge(S["maxrow_loaded"][vp], 16 * 2 * MROWS * i_prev)
                nc.vector.tensor_copy(mrow[vp][:, :],
                                      PS[0:4 * MROWS, RB + TSLOT % RING, :].bitcast(BF16)
                                      ).then_inc(S["row_read"], 1)

            def body(u, p, i):
                for s in range(pl.n):
                    for v, r in pl.stream(u, s):
                        if r is None:
                            _, vp, vi = ahead(u, p, i, 1)
                            rows_of_max(v, vp, vi, v + 1)
                        else:
                            d = 1 if s + LEAD < pl.n else 2
                            row_max(v, (p + d) % 2, r)

            for r in range(pl.nr):
                row_max(0, 0, r)
            for r in range(TSLOT):
                row_max(1, 1, r)
            rows_of_max(0, 0, 0, 1)
            for r in range(TSLOT, 4 * LEAD):
                row_max(1, 1, r)
            pairwise(dve, body)

        def att_act(act, a):
            S, pl = att[a], plans[a]

            def exps(u, s, g):
                c, kt = pl.steps[s]
                off = pl.off(c, kt)
                ready, signal = (S["scores_a"], S["exp_a"]) if g == 0 else (S["scores_b"], S["exp_b"])
                if g == 0:
                    wait(act, S["pv_done"], pl.n * u + s - 1)
                act.wait_ge(ready, pl.n * u + s + 1)
                nc.scalar.activation(PR[s % 2][:, 2 * g:2 * g + 2, off:CH],
                                     PS[:, TB + 2 * g:TB + 2 * g + 2, off:CH], ACT.Exp).then_inc(signal, 1)

            def copy_outputs(u, c):
                ends = [s for s in range(pl.n) if pl.last(s)]
                act.wait_ge(S["pv_done"], pl.n * u + ends[c] + 1)
                wait(act, S["o_stored"][c], 64 * u)
                nc.scalar.copy(OS[c][:, :], PS[:, AC, :]).then_inc(S["acc_copied"], 1)

            def body(u, p, i):
                for s in range(pl.n):
                    exps(u, s, 0)
                    exps(u, s, 1)
                    if s == 0 and not (isinstance(u, int) and u == 0):
                        copy_outputs(u - 1, NC - 1)
                    if s > 0 and pl.last(s - 1):
                        copy_outputs(u, pl.steps[s - 1][0])

            pairwise(act, body)
            copy_outputs(UNITS - 1, NC - 1)

        def att_sp(sp, a):
            S, pl = att[a], plans[a]

            def load_stacks(u, q_dst, k_dst, signal):
                for st, dst in ((q_st[a], q_dst), (k_st[a], k_dst)):
                    for hp in range(2):
                        buf = dst[hp] if isinstance(dst, list) else dst
                        sp.dma_start(buf[64 * hp:64 * hp + ROWS, :, :],
                                     st.rearrange("u (g r) c d n -> u r (c d) g n", r=2)[u][hp]
                                     ).then_inc(signal, 16)

            def load_main(u, p):
                load_stacks(u, QS[p], KS[p], S["main_loaded"][p])
                sp.dma_start(VS[p][:, :, 0:VW], v_st[a].rearrange("u (t p) w -> u p t w", p=P)[u]
                             ).then_inc(S["main_loaded"][p], 16)

            def load_row(u, p):
                load_stacks(u, QR[p], KR[p], S["row_loaded"][p])

            def load_maxima(u, p):
                sp.wait_ge(S["row_read"], pl.used(u + 1, TSLOT))
                for hp in range(2):
                    for m in range(MROWS):
                        row = 2 * MROWS * hp + 2 * m
                        sp.dma_start(QS[p][64 * hp + ROWS + m:64 * hp + ROWS + m + 1, :, :],
                                     mrow[p][row:row + 2, :]).then_inc(S["maxrow_loaded"][p], 16)

            def store(u, c):
                sp.wait_ge(S["acc_copied"], NC * u + c + 1)
                for h in range(HG):
                    sp.dma_start(o_st[a][u][h, :, c * CH:(c + 1) * CH], OS[c][32 * h:32 * h + HD + 1, :]
                                 ).then_inc(S["o_stored"][c], 16)

            def body(u, p, i):
                last = isinstance(u, int) and u + 1 >= UNITS
                if not last:
                    sp.wait_ge(S["scores_a"], pl.n * u + 2)
                    load_main(u + 1, 1 - p)
                if not (isinstance(u, int) and u + 2 >= UNITS):
                    sp.wait_ge(S["row_ready"], pl.used(u, pl.nr))
                    load_row(u + 2, p)
                store(u, 0)
                if not last:
                    load_maxima(u + 1, 1 - p)
                store(u, 1)

            load_row(0, 0)
            load_main(0, 0)
            load_row(1, 1)
            load_maxima(0, 0)
            pairwise(sp, body)
            for c in range(NC):
                sp.wait_ge(S["o_stored"][c], 64 * UNITS)

        def load_outputs(sp, S, a, b):
            view = o_st[a].rearrange("(b u) j r n -> b (u j) r n", u=UPB)[b]
            sp.dma_start(oT[:, :], view[:, 0:HD, :]).then_inc(S["o_loaded"], 16)
            for h in range(H):
                sp.dma_start(lB[HD * h:HD * h + HD, :], view[h, HD:HD + 1, :].to_broadcast([HD, N])
                             ).then_inc(S["l_loaded"], 16)

        MID_CHAIN = 11

        def mid_sp(sp):
            S = mid
            with sp.Fori(0, B) as b:
                sp.wait_ge(S["on_free"], b + 1)
                load_outputs(sp, S, 0, b)

        def mid_dve(dve):
            S = mid
            dve.sem_inc(S["on_free"], 1)
            with dve.Fori(0, B) as b:
                ch = Chain(dve, S["chain"], b * MID_CHAIN)
                dve.wait_ge(S["l_loaded"], 16 * H * (b + 1))
                ch.link(nc.vector.reciprocal(lB[:, :], lB[:, :]))
                dve.wait_ge(S["o_loaded"], 16 * (b + 1))
                nc.vector.tensor_tensor(oN[:, :], oT[:, :], lB[:, :], ALU.mult).then_inc(S["on_ready"], 1)
                dve.wait_ge(S["on_ready"], b + 1)
                dve.sem_inc(S["on_free"], 1)
                dve.wait_ge(S["on_psum"], b + 1)
                norm_stats(dve, ch, psum_tile(0), S, 2 * b + 1)
                normalise(nat, psum_tile(0)).then_inc(S["ln_ready"], 1)
                dve.wait_ge(S["y_psum"], b + 1)
                ch.link(nc.vector.tensor_tensor(tiles(nat2), banks(4), wide(bo_s[0]), ALU.add))
                norm_stats(dve, ch, tile(nat2), S, 2 * b + 2)
                ch.link(normalise(nat2, tile(nat2)))
                nc.vector.tensor_tensor(X[:, b, :], X[:, b, :], nat2[:, :], ALU.add).then_inc(S["x_ready"], 1)
                assert ch.n == MID_CHAIN, ch.n
            dve.wait_ge(S["x_ready"], B)

        def mid_act(act):
            S = mid
            with act.Fori(0, B) as b:
                root(act, S, 2 * b + 1)
                act.wait_ge(S["ln_psum"], b + 1)
                for c in range(2):
                    ins = nc.scalar.activation(xT[:, c * CH:(c + 1) * CH], PS[:, 2 + c, :], ACT.Identity,
                                               scale=lng_s[:, :], bias=lnb_s[:, :])
                ins.then_inc(S["lnt_ready"], 1)
                root(act, S, 2 * b + 2)

        def mid_pe(pe):
            S = mid
            with pe.Fori(0, B) as b:
                pe.wait_ge(S["on_ready"], b + 1)
                for t in range(NT):
                    ins = nc.tensor.transpose(PS[:, t // 4, (t % 4) * P:(t % 4 + 1) * P],
                                              oN[:, t * P:(t + 1) * P], ident[:, :])
                ins.then_inc(S["on_psum"], 1)
                pe.wait_ge(S["ln_ready"], b + 1)
                for t in range(NT):
                    ins = nc.tensor.transpose(PS[:, 2 + t // 4, (t % 4) * P:(t % 4 + 1) * P],
                                              nat[:, t * D:(t + 1) * D], ident[:, :])
                ins.then_inc(S["ln_psum"], 1)
                pe.wait_ge(S["lnt_ready"], b + 1)
                for t in range(NT):
                    ins = nc.tensor.matmul(PS[:, 4 + t // 4, (t % 4) * D:(t % 4 + 1) * D],
                                           xT[:, t * P:(t + 1) * P], wo_s[0][:, :], start=True, stop=True)
                ins.then_inc(S["y_psum"], 1)

        TAIL_CHAIN = 33

        def tail_sp(sp):
            S = tail
            with sp.Fori(0, B) as b:
                sp.wait_ge(S["on_free"], b + 1)
                load_outputs(sp, S, 1, b)
                sp.wait_ge(S["out_ready"], b + 1)
                sp.dma_start(out_d.rearrange("b (t p) d -> b p t d", p=P)[b], tiles(res)
                             ).then_inc(S["out_stored"], 16)
            sp.wait_ge(S["out_stored"], 1 + 16 * B)

        def tail_dve(dve):
            S = tail
            dve.sem_inc(S["on_free"], 1)
            dve.sem_inc(S["out_stored"], 1)
            with dve.Fori(0, B) as b:
                ch = Chain(dve, S["chain"], b * TAIL_CHAIN)
                V = nc.vector
                dve.wait_ge(S["l_loaded"], 16 * H * (b + 1))
                ch.link(V.reciprocal(lB[:, :], lB[:, :]))
                dve.wait_ge(S["o_loaded"], 16 * (b + 1))
                V.tensor_tensor(oN[:, :], oT[:, :], lB[:, :], ALU.mult).then_inc(S["on_ready"], 1)
                dve.wait_ge(S["on_ready"], b + 1)
                dve.sem_inc(S["on_free"], 1)
                dve.wait_ge(S["y_psum"], b + 1)
                ch.link(V.tensor_tensor(tiles(nat2), banks(4), wide(bo_s[1]), ALU.add))
                ch.link(V.tensor_tensor(nat2[:, :], nat2[:, :], XH[:, b, :], ALU.add))
                norm_stats(dve, ch, tile(nat2), S, 3 * b + 1)
                ch.link(normalise(nat, tile(nat2)))
                ch.link(V.tensor_tensor(tiles(nat), tiles(nat), wide(l1g_s), ALU.mult))
                V.tensor_tensor(tiles(nat), tiles(nat), wide(l1b_s), ALU.add).then_inc(S["xf_ready"], 1)
                dve.wait_ge(S["logit_psum"], b + 1)
                rows = lambda v: v[:, :].rearrange("p (t a) -> p t a", a=1).to_broadcast([P, NT, E])
                ch.link(V.tensor_tensor(lg[:, :, :], PS[:, 6, 0:NT * E].rearrange("p (t e) -> p t e", e=E),
                                        gb_s[:, :].rearrange("p (a e) -> p a e", a=1).to_broadcast([P, NT, E]),
                                        ALU.add))
                ch.link(V.reduce_max(gs[:, :], lg[:, :, :], AX.X))
                V.tensor_tensor(lg[:, :, :], lg[:, :, :], rows(gs), ALU.subtract).then_inc(S["shifted"], 1)
                dve.wait_ge(S["exp_ready"], b + 1)
                ch.link(V.reduce_sum(gs[:, :], ge[:, :, :], AX.X))
                ch.link(V.reciprocal(gs[:, :], gs[:, :]))
                ch.link(V.tensor_tensor(ge[:, :, :], ge[:, :, :], rows(gs), ALU.mult))
                this = ge[:, :, :].rearrange("p t (e a) -> p t e a", a=1).to_broadcast([P, NT, E, E])
                other = ge[:, :, :].rearrange("p t (a e) -> p t a e", a=1).to_broadcast([P, NT, E, E])
                before = before_e[:, :, :].rearrange("p (a e) f -> p a e f", a=1).to_broadcast([P, NT, E, E])
                ch.link(V.tensor_tensor(cmp1[:, :, :, :], other, this, ALU.is_gt))
                ch.link(V.tensor_tensor(cmp2[:, :, :, :], other, this, ALU.is_equal))
                ch.link(V.tensor_tensor(cmp2[:, :, :, :], cmp2[:, :, :, :], before, ALU.mult))
                ch.link(V.tensor_tensor(cmp1[:, :, :, :], cmp1[:, :, :, :], cmp2[:, :, :, :], ALU.add))
                ch.link(V.reduce_sum(lg[:, :, :], cmp1[:, :, :, :], AX.X))
                V.scalar_tensor_tensor(wt[:, :, :], lg[:, :, :], 2.0, ge[:, :, :], ALU.is_lt,
                                       ALU.mult).then_inc(S["wt_ready"], 1)
                for c in range(NC):
                    dve.wait_ge(S["bias_psum"], NC * b + c + 1)
                    part = slice(c * CH, (c + 1) * CH)
                    ch.link(V.tensor_tensor(nat2[:, part], nat[:, part], PS[:, 6, :], ALU.add))
                    for e in range(E):
                        dve.wait_ge(S["e_psum"], E * (NC * b + c) + e + 1)
                        for t in range(4):
                            tt = 4 * c + t
                            y = nat2[:, tt * D:(tt + 1) * D]
                            ins = V.scalar_tensor_tensor(y, PS[:, 4 + e % 2, t * D:(t + 1) * D],
                                                         wt[:, tt, e:e + 1], y, ALU.mult, ALU.add)
                        ins.then_inc(S["e_added"], 1)
                        dve.wait_ge(S["e_added"], E * (NC * b + c) + e + 1)
                norm_stats(dve, ch, tile(nat2), S, 3 * b + 2)
                ch.link(normalise(nat2, tile(nat2)))
                ch.link(V.tensor_tensor(tiles(nat2), tiles(nat2), wide(l2g_s), ALU.mult))
                ch.link(V.tensor_tensor(tiles(nat2), tiles(nat2), wide(l2b_s), ALU.add))
                norm_stats(dve, ch, tile(nat2), S, 3 * b + 3)
                ch.link(normalise(nat2, tile(nat2)))
                dve.wait_ge(S["out_stored"], 16 * b + 1)
                V.tensor_tensor(res[:, :], nat2[:, :], X[:, b, :], ALU.add).then_inc(S["out_ready"], 1)
                assert ch.n == TAIL_CHAIN, ch.n

        def tail_act(act):
            S = tail
            with act.Fori(0, B) as b:
                root(act, S, 3 * b + 1)
                act.wait_ge(S["xf_psum"], b + 1)
                for c in range(2):
                    ins = nc.scalar.copy(xT[:, c * CH:(c + 1) * CH], PS[:, c, :])
                ins.then_inc(S["xt_ready"], 1)
                act.wait_ge(S["shifted"], b + 1)
                nc.scalar.activation(ge[:, :, :], lg[:, :, :], ACT.Exp).then_inc(S["exp_ready"], 1)
                act.wait_ge(S["wt_psum"], b + 1)
                nc.scalar.copy(wT[:, :], PS[0:E, 2:4, :]).then_inc(S["wT_ready"], 1)
                for n in range(NC * E):
                    e = n % E
                    act.wait_ge(S["h_psum"], NC * E * b + n + 1)
                    for f in range(2):
                        ins = nc.scalar.activation(hT[e % 2][:, f, :], PS[:, 2 * (e % 2) + f, :], ACT.Relu,
                                                   bias=b1_s[:, e, f:f + 1])
                    ins.then_inc(S["h_ready"], 1)
                root(act, S, 3 * b + 2)
                root(act, S, 3 * b + 3)

        def tail_pe(pe):
            S = tail
            with pe.Fori(0, B) as b:
                pe.wait_ge(S["on_ready"], b + 1)
                for t in range(NT):
                    ins = nc.tensor.matmul(PS[:, 4 + t // 4, (t % 4) * D:(t % 4 + 1) * D],
                                           oN[:, t * P:(t + 1) * P], wo_s[1][:, :], start=True, stop=True)
                ins.then_inc(S["y_psum"], 1)
                pe.wait_ge(S["xf_ready"], b + 1)
                for t in range(NT):
                    ins = nc.tensor.transpose(PS[:, t // 4, (t % 4) * P:(t % 4 + 1) * P],
                                              nat[:, t * D:(t + 1) * D], ident[:, :])
                ins.then_inc(S["xf_psum"], 1)
                pe.wait_ge(S["xt_ready"], b + 1)
                for t in range(NT):
                    ins = nc.tensor.matmul(PS[:, 6, t * E:(t + 1) * E], xT[:, t * P:(t + 1) * P], gw_s[:, :],
                                           start=True, stop=True)
                ins.then_inc(S["logit_psum"], 1)
                pe.wait_ge(S["wt_ready"], b + 1)
                for t in range(NT):
                    ins = nc.tensor.transpose(PS[0:E, 2 + t // 4, (t % 4) * P:(t % 4 + 1) * P],
                                              wt[:, t, :], ident[:, :])
                ins.then_inc(S["wt_psum"], 1)
                pe.wait_ge(S["wT_ready"], b + 1)

                def hidden(n):
                    c, e = n // E, n % E
                    for f in range(2):
                        ins = nc.tensor.matmul(PS[:, 2 * (e % 2) + f, :], w1_s[:, e, f * P:(f + 1) * P],
                                               xT[:, c * CH:(c + 1) * CH], start=True, stop=True)
                    ins.then_inc(S["h_psum"], 1)

                def second(n):
                    c, e = n // E, n % E
                    pe.wait_ge(S["h_ready"], NC * E * b + n + 1)
                    if n >= 2:
                        pe.wait_ge(S["e_added"], NC * E * b + n - 1)
                    for t in range(4):
                        for f in range(2):
                            ins = nc.tensor.matmul(PS[:, 4 + e % 2, t * D:(t + 1) * D],
                                                   hT[e % 2][:, f, t * P:(t + 1) * P], w2_s[:, e, f, :],
                                                   start=f == 0, stop=f == 1)
                    ins.then_inc(S["e_psum"], 1)

                def bias(c):
                    if c:
                        pe.wait_ge(S["e_added"], NC * E * b + 1 + E * (c - 1))
                    for t in range(4):
                        tt = 4 * c + t
                        ins = nc.tensor.matmul(PS[:, 6, t * D:(t + 1) * D], wT[:, tt * P:(tt + 1) * P],
                                               b2_s[:, :], start=True, stop=True)
                    ins.then_inc(S["bias_psum"], 1)

                hidden(0)
                for n in range(NC * E):
                    if n % E == 0:
                        bias(n // E)
                    if n + 1 < NC * E:
                        hidden(n + 1)
                    second(n)

        @block.sync
        def _(sp):
            for dst, src in loads:
                sp.dma_start(dst, src, allow_slow_non_contiguous=True).then_inc(wload, 16)
            prep_sp(sp, 0)
            att_sp(sp, 0)
            mid_sp(sp)
            prep_sp(sp, 1)
            att_sp(sp, 1)
            tail_sp(sp)

        @block.vector
        def _(dve):
            for p in range(2):
                nc.vector.memset(mx[p][:, :, :, :], 3e38)
                nc.vector.memset(VS[p][:, :, :], 0.0)
                for h in range(2):
                    nc.vector.memset(KS[p][h][64 * h:64 * h + 64, :, :], 1.0)
                    for buf in (KS[p][h], QR[p][h]):
                        half = buf[64 - 64 * h:128 - 64 * h, :, :]
                        nc.vector.memset(half, 0.0)
                    nc.vector.memset(QR[p][h][64 * h:64 * h + 64, :, :], 0.0)
                for buf in (QS[p], KR[p]):
                    nc.vector.memset(buf[:, :, :], 0.0)
            nc.vector.memset(vsb[:, :, :, :], 1.0)
            nc.vector.memset(before_e[:, :, :], 0.0).then_inc(const_dve, 1)
            dve.wait_ge(const_dve, 1)
            for e in range(1, E):
                ins = nc.vector.memset(before_e[:, e, 0:e], 1.0)
            ins.then_inc(const_dve, 1)
            dve.wait_ge(const_dve, 2)
            dve.wait_ge(wload, LOADED)
            prep_dve(dve, 0)
            att_dve(dve, 0)
            mid_dve(dve)
            prep_dve(dve, 1)
            att_dve(dve, 1)
            tail_dve(dve)

        @block.scalar
        def _(act):
            act.wait_ge(wload, LOADED)
            prep_act(act, 0)
            att_act(act, 0)
            mid_act(act)
            prep_act(act, 1)
            att_act(act, 1)
            tail_act(act)

        @block.gpsimd
        def _(pool):
            nc.gpsimd.memset(ident[:, :], 0.0)
            nc.gpsimd.memset(mask_q[:, :], 0.0)
            nc.gpsimd.memset(mask_k[:, :], 0.0).then_inc(const_ready, 1)
            pool.wait_ge(const_ready, 1)
            nc.gpsimd.affine_select(out=ident[:, :], in_=ident[:, :], compare_op=ALU.not_equal, fill=1.0,
                                    base=0, pattern=[[-1, P]], channel_multiplier=1)
            nc.gpsimd.affine_select(out=mask_q[:, :], in_=mask_q[:, :], compare_op=ALU.is_ge, fill=NEG,
                                    base=0, pattern=[[-1, P]], channel_multiplier=1)
            nc.gpsimd.affine_select(out=mask_k[:, :], in_=mask_k[:, :], compare_op=ALU.is_ge, fill=NEG,
                                    base=0, pattern=[[1, P]], channel_multiplier=-1).then_inc(const_ready, 1)
            pool.wait_ge(const_ready, 2)
            nc.gpsimd.tensor_copy(identb[:, :], ident[:, :]).then_inc(const_ready, 1)
            prep_pool(pool, 0)
            prep_pool(pool, 1)

        @block.tensor
        def _(pe):
            pe.wait_ge(wload, LOADED)
            pe.wait_ge(const_ready, 3)
            prep_pe(pe, 0)
            att_pe(pe, 0)
            mid_pe(pe)
            prep_pe(pe, 1)
            att_pe(pe, 1)
            tail_pe(pe)


_INS = ["L0_attn_x"] + ["L0_attn_" + n for n in "Wq bq Wk bk Wv bv ln_g ln_b Wo bo".split()] + \
       ["L0_ffn_" + n for n in "Wq bq Wk bk Wv bv Wo bo gW gb W1 b1 W2 b2 ln1_g ln1_b ln2_g ln2_b".split()]


def kernel(**inputs):
    import numpy as _np
    import concourse.bacc as _bacc
    from concourse import mybir as _mybir
    from concourse.bass_utils import run_bass_kernel_spmd as _run

    nc = _bacc.Bacc("TRN2", target_bir_lowering=False, num_devices=1)
    arrays, args = {}, []
    for name in _INS:
        a = _np.ascontiguousarray(inputs[name])
        arrays[f"in_{name}_dram"] = a
        args.append(nc.dram_tensor(f"in_{name}_dram", a.shape, _mybir.dt.from_np(a.dtype), kind="ExternalInput").ap())
    args.append(nc.dram_tensor("out_0_dram", (B, N, D), _mybir.dt.float32, kind="ExternalOutput").ap())
    sandwich(nc, *args)
    r = _run(nc, [arrays], core_ids=[0])
    return r.results[0]["out_0_dram"]
```

```python
import concourse.bass as bass
from concourse import mybir
from contextlib import ExitStack

FP32 = mybir.dt.float32
BF16 = mybir.dt.bfloat16
ALU = mybir.AluOpType
ACT = mybir.ActivationFunctionType
AX = mybir.AxisListType

B, N, D = 4, 1024, 128
P = 128
H, HD = 16, 8
KVH = 4
E, FF = 8, 256
NT = N // P
HG = 4
UNITS = B * H // HG
UPB = H // HG
CH = 512
NC = N // CH
QPARTS = [0, 0, 0, 1, 1, 2]
KPARTS = [0, 1, 2, 0, 1, 0]
NB = len(QPARTS)
ROWS = NB * HD
MROWS = 3
VW = HG * (HD + 1)
VPAD = 60
SCALE = float(HD) ** -0.5
EPS = 1e-5
NEG = -1e30
LEAD = 4
RING = 3
PRING = 4
TSLOT = 4


def wait(eng, sem, value):
    if isinstance(value, int) and value <= 0:
        return
    eng.wait_ge(sem, value)


class Plan:

    def __init__(self, causal):
        self.causal = causal
        self.steps = [(c, kt) for c in range(NC) for kt in range(NT)
                      if not causal or kt * P < (c + 1) * CH]
        self.n = len(self.steps)
        self.rows = []
        for qt in range(NT):
            for half in range(NC):
                width = min(CH, (qt + 1) * P - half * CH) if causal else CH
                if width > 0:
                    self.rows += [(qt, half, width, g, r) for g in range(2) for r in range(2)]
        self.nr = len(self.rows)
        self.per = self.nr // self.n
        assert self.per == 4 and self.nr == 4 * self.n
        self.used_slots = self.nr + 1
        self.slots = -(-self.used_slots // RING) * RING

    def off(self, c, kt):
        return max(0, kt * P - c * CH) if self.causal else 0

    def first(self, c, kt):
        return kt == 0

    def last(self, s):
        return s == self.n - 1 or self.steps[s + 1][0] != self.steps[s][0]

    def slot_of(self, r):
        return r if r < TSLOT else r + 1

    def used(self, v, x):
        if isinstance(v, int) and v == 0 and x < TSLOT:
            return x + 1
        if isinstance(v, int) and v == UNITS:
            return v * self.used_slots
        return v * self.used_slots + x

    def before(self, v, x):
        alone = isinstance(v, int) and v == UNITS
        if x >= RING and not alone:
            return self.used(v, x - RING)
        y = self.slots - RING + x % RING
        while y > self.nr:
            y -= RING
        if isinstance(v, int) and v == 0:
            return 0
        return self.used(v - 1, y)

    def stream(self, u, s):
        t = s + LEAD
        v, base = (u + 1, 4 * t) if t < self.n else (u + 2, 4 * (t - self.n))
        over = isinstance(v, int) and v >= UNITS
        out = []
        for r in range(base, base + 4):
            if r == TSLOT and (not isinstance(v, int) or v <= UNITS):
                out.append((v - 1, None))
            if not over:
                out.append((v, r))
        return out


def sandwich(nc, x_d, wq1, bq1, wk1, bk1, wv1, bv1, lng1, lnb1, wo1, bo1,
             wq2, bq2, wk2, bk2, wv2, bv2, wo2, bo2, gw, gb, w1, b1, w2, b2,
             l1g, l1b, l2g, l2b, out_d):
    ctx = ExitStack()

    def sb(name, shape, dt=FP32):
        return ctx.enter_context(nc.sbuf_tensor(name, shape, dt))

    def dram(name, shape, dt):
        return nc.dram_tensor(name, shape, dt, kind="Internal").ap()

    def sem(name):
        return ctx.enter_context(nc.semaphore(name))

    with ctx:
        q_st = [dram(f"q_st{a}", (UNITS, HG, NB, HD, N), BF16) for a in range(2)]
        k_st = [dram(f"k_st{a}", (UNITS, HG, NB, HD, N), BF16) for a in range(2)]
        v_st = [dram(f"v_st{a}", (UNITS, N, VW), FP32) for a in range(2)]
        o_st = [dram(f"o_st{a}", (UNITS, HG, HD + 1, N), FP32) for a in range(2)]

        wq_s = [sb(f"wq{a}", [P, D]) for a in range(2)]
        wk_s = [sb(f"wk{a}", [P, D]) for a in range(2)]
        wv_s = [sb(f"wv{a}", [P, D]) for a in range(2)]
        wo_s = [sb(f"wo{a}", [P, D]) for a in range(2)]
        bq_s = [sb(f"bq{a}", [P, 1]) for a in range(2)]
        bk_s = [sb(f"bk{a}", [P, 1]) for a in range(2)]
        bv_s = [sb(f"bv{a}", [P, D]) for a in range(2)]
        bo_s = [sb(f"bo{a}", [P, D]) for a in range(2)]
        lng_s, lnb_s = sb("lng", [P, 1]), sb("lnb", [P, 1])
        gw_s, gb_s = sb("gw", [P, E]), sb("gb", [P, E])
        w1_s, b1_s = sb("w1", [P, E, FF]), sb("b1", [P, E, 2])
        w2_s, b2_s = sb("w2", [P, E, 2, D]), sb("b2", [E, D])
        l1g_s, l1b_s = sb("l1g", [P, D]), sb("l1b", [P, D])
        l2g_s, l2b_s = sb("l2g", [P, D]), sb("l2b", [P, D])
        ident = sb("ident", [P, P])
        identb = sb("identb", [P, P], BF16)
        mask_q = sb("mask_q", [P, P], BF16)
        mask_k = sb("mask_k", [P, P], BF16)
        before_e = sb("before_e", [P, E, E])

        X = sb("X", [P, B, NT * D])
        XH = sb("XH", [P, B, NT * D])
        xT = sb("xT", [P, N])
        nat = sb("nat", [P, NT * D])
        nat2 = sb("nat2", [P, NT * D])
        bnst = sb("bnst", [P, NT, 6])
        mean, dif = sb("mean", [P, NT]), sb("dif", [P, NT])
        std = sb("std", [P, NT])
        rstd = sb("rstd", [P, NT])
        qf = [sb("qf", [P, N]), sb("kf", [P, N])]
        parts = [[sb(f"part{t}{j}", [P, N], BF16) for j in range(3)] for t in range(2)]
        vsb = sb("vsb", [P, NT, H, HD + 1])
        oT, lT, rl = sb("oT", [P, N]), sb("lT", [H, N]), sb("rl", [P, NT * H])
        bqs_s = [sb(f"bqs{a}", [P, 1]) for a in range(2)]
        res, div = sb("res", [P, NT * D]), sb("div", [P, NT * D])
        QS = [sb(f"QS{p}", [P, 2, N], BF16) for p in range(2)]
        KS = [[sb(f"KS{p}{h}", [P, 2, N], BF16) for h in range(2)] for p in range(2)]
        QR = [[sb(f"QR{p}{h}", [P, 2, N], BF16) for h in range(2)] for p in range(2)]
        KR = [sb(f"KR{p}", [P, 2, N], BF16) for p in range(2)]
        VS = [sb(f"VS{p}", [P, NT, VPAD]) for p in range(2)]
        PR = [sb(f"PR{p}", [P, HG, CH]) for p in range(PRING)]
        OS = [sb(f"OS{c}", [P, CH]) for c in range(NC)]
        mx = [sb(f"mx{p}", [P, NT, 4, 2]) for p in range(2)]
        nm, nm2 = sb("nm", [P, NT * 4]), sb("nm2", [P, NT * 4])
        mparts = [sb(f"mparts{p}", [P, NT, 2, MROWS, 2], BF16) for p in range(2)]
        mrow = [sb(f"mrow{p}", [4 * MROWS, N], BF16) for p in range(2)]
        flat = lambda buf, k: buf[:, 2 * k:2 * k + 2, :].rearrange("p a n -> p (a n)")
        lg, ge = sb("lg", [P, NT, E]), sb("ge", [P, NT, E])
        wt = [sb(f"wt{p}", [P, NT, E]) for p in range(2)]
        gs = sb("gs", [P, NT])
        acc = [flat(PR[0], k) for k in range(2)]
        hT = [PR[1][:, 2 * k:2 * k + 2, :] for k in range(2)]
        cmp1, cmp2 = (PR[2][:, k, :].rearrange("p (t e f) -> p t e f", t=NT, e=E) for k in range(2))
        oN = flat(PR[2], 1)
        xTs = [xT[:, :], flat(PR[3], 0)]
        wT = flat(PR[3], 1)[0:E, :]
        xf = [nat, nat2]

        PS = ctx.enter_context(nc.psum_tensor("PS", [P, 8, CH], FP32))
        TB = 0
        AC = 4
        RB = 5

        x_loaded = [sem("x_first_loaded"), sem("x_rest_loaded")]
        weights_loaded = [sem(f"weights{a}_loaded") for a in range(2)]
        const_ready = sem("const_ready")
        const_dve = sem("const_dve")
        cleared, CLEARED = sem("cleared"), 4
        block = ctx.enter_context(nc.Block())

        x_view = x_d.rearrange("b (t p) d -> b p t d", p=P)
        loads = [[], []]
        col = lambda v: v.rearrange("(p a) -> p a", a=1)
        bc = lambda v, n: v.rearrange("(a n) -> a n", a=1).to_broadcast([P, n])
        for a, (wq, wk, wv, bq, bk, bv) in enumerate([(wq1, wk1, wv1, bq1, bk1, bv1),
                                                      (wq2, wk2, wv2, bq2, bk2, bv2)]):
            loads[a] += [(wq_s[a][:, :], wq), (bq_s[a][:, :], col(bq))]
            kv = wk.shape[1]
            for c in range(0, D, kv):
                loads[a] += [(wk_s[a][:, c:c + kv], wk), (bk_s[a][c:c + kv, :], col(bk)),
                             (wv_s[a][:, c:c + kv], wv), (bv_s[a][:, c:c + kv], bc(bv, kv))]
        loads[1] += [(wo_s[0][:, :], wo1), (wo_s[1][:, :], wo2), (bo_s[0][:, :], bc(bo1, D)),
                     (bo_s[1][:, :], bc(bo2, D)), (lng_s[:, :], col(lng1)), (lnb_s[:, :], col(lnb1)),
                     (gw_s[:, :], gw), (gb_s[:, :], bc(gb, E)), (b2_s[:, :], b2),
                     (w1_s[:, :, :], w1.rearrange("e d f -> d e f"))]
        for e in range(E):
            loads[1] += [(b1_s[:, e, :], b1[e].rearrange("(a f) -> f a", a=2)),
                         (w2_s[:, e, :, :], w2[e].rearrange("(a f) d -> f a d", a=2))]
        loads[1] += [(dst[:, :], bc(src, D)) for dst, src in
                     ((l1g_s, l1g), (l1b_s, l1b), (l2g_s, l2g), (l2b_s, l2b))]
        LOADED = [16 * len(part) for part in loads]

        def signals(phase, names):
            return {name: sem(f"{phase}_{name}") for name in names.split()}

        PREP = ("chain ol_loaded ol_psum o_ready var_ready std_ready ln_ready ln_psum lnt_ready y_psum "
                "bqs_ready x_ready x_kept xh_ready xh_kept xt_psum xt_ready q_psum k_psum v_psum q_taken k_taken "
                "q_rounded k_rounded q_rest k_rest q_parts k_parts v_ready qst_stored kst_stored vst_stored")
        prep = [signals(f"prep{a}", PREP) for a in range(2)]
        TAIL = ("chain ol_loaded ol_psum o_ready on_psum on_ready y_psum var_ready std_ready xf_ready "
                "xf_psum xt_ready logit_psum shifted exp_ready wt_ready wt_psum wT_ready bias_psum "
                "acc_begun h_psum h_ready e_psum e_added out_ready out_stored")
        tail = signals("tail", TAIL)
        ATT = ("row_ready row_read chain max_ready scores_a scores_b exp_a exp_b pv_done "
               "acc_copied")
        att = [signals(f"att{a}", ATT) for a in range(2)]
        for a in range(2):
            for name, n in (("row_loaded", 2), ("main_loaded", 2), ("maxrow_loaded", 2), ("o_stored", NC)):
                att[a][name] = [sem(f"att{a}_{name}{p}") for p in range(n)]
        plans = [Plan(True), Plan(False)]

        class Chain:

            def __init__(self, eng, counts, base):
                self.eng, self.counts, self.base, self.n = eng, counts, base, 0

            def link(self, ins):
                self.n += 1
                ins.then_inc(self.counts, 1)
                self.eng.wait_ge(self.counts, self.base + self.n)

        def variance(chain, src, S):
            for t in range(NT):
                ins = nc.vector.bn_stats(bnst[:, t, :], src(t))
            chain.link(ins)
            mean_e, sq_e, mean_o, sq_o = (bnst[:, :, k] for k in (1, 2, 4, 5))
            nc.vector.tensor_tensor(mean[:, :], mean_e, mean_o, ALU.add)
            nc.vector.tensor_tensor(dif[:, :], mean_e, mean_o, ALU.subtract)
            chain.link(nc.vector.scalar_tensor_tensor(std[:, :], sq_e, D * EPS, sq_o, ALU.add, ALU.add))
            nc.vector.tensor_scalar(mean[:, :], mean[:, :], 0.5, None, ALU.mult)
            chain.link(nc.vector.scalar_tensor_tensor(dif[:, :], dif[:, :], D / 4.0, dif[:, :],
                                                      ALU.mult, ALU.mult))
            nc.vector.tensor_tensor(std[:, :], std[:, :], dif[:, :], ALU.add).then_inc(S["var_ready"], 1)

        def deviation(dve, chain, S, at):
            dve.wait_ge(S["std_ready"], at)
            chain.link(nc.vector.reciprocal(rstd[:, :], std[:, :]))

        def norm_stats(dve, chain, src, S, at):
            variance(chain, src, S)
            deviation(dve, chain, S, at)

        def root(act, S, at):
            act.wait_ge(S["var_ready"], at)
            nc.scalar.activation(std[:, :], std[:, :], ACT.Sqrt, scale=1.0 / D).then_inc(S["std_ready"], 1)

        def normalise(dst, src):
            for t in range(NT):
                ins = nc.vector.tensor_scalar(dst[:, t * D:(t + 1) * D], src(t),
                                              mean[:, t:t + 1], rstd[:, t:t + 1], ALU.subtract, ALU.mult)
            return ins

        def tile(buf):
            return lambda t: buf[:, t * D:(t + 1) * D]

        def psum_tile(bank):
            return lambda t: PS[:, bank + t // 4, (t % 4) * D:(t % 4 + 1) * D]

        def wide(v):
            return v[:, :].rearrange("p (a d) -> p a d", a=1).to_broadcast([P, NT, D])

        def banks(bank):
            return PS[:, bank:bank + 2, :].rearrange("p c (t d) -> p (c t) d", d=D)

        def tiles(buf):
            return buf[:, :].rearrange("p (t d) -> p t d", d=D)

        def spread(x):
            return x.rearrange("p (t d) -> p t d", d=D)

        def divide(chain, o_banks, l_bank, signal):
            chain.link(nc.vector.reciprocal(rl[:, :], PS[:, l_bank, 0:NT * H]))
            nc.vector.tensor_tensor(
                div[:, :].rearrange("p (h d) -> p h d", d=HD),
                PS[:, o_banks:o_banks + 2, :].rearrange("p c (h d) -> p (c h) d", d=HD),
                rl[:, :].rearrange("p (h a) -> p h a", a=1).to_broadcast([P, NT * H, HD]),
                ALU.mult).then_inc(signal, 1)

        def transpose_tiles(bank, src):
            for t in range(NT):
                ins = nc.tensor.transpose(PS[:, bank + t // 4, (t % 4) * P:(t % 4 + 1) * P],
                                          src[:, t * P:(t + 1) * P], ident[:, :])
            return ins

        def transpose_outputs(o_banks, l_bank):
            transpose_tiles(o_banks, oT)
            for t in range(NT):
                ins = nc.tensor.transpose(PS[:, l_bank, t * H:(t + 1) * H], lT[:, t * P:(t + 1) * P],
                                          ident[0:H, 0:H])
            return ins

        def load_outputs(sp, signal, a, b):
            view = o_st[a].rearrange("(b u) j r n -> b (u j) r n", u=UPB)[b]
            sp.dma_start(oT[:, :], view[:, 0:HD, :]).then_inc(signal, 16)
            sp.dma_start(lT[:, :], view[:, HD, :]).then_inc(signal, 16)

        def batches(eng, body):
            body(0, True)
            with eng.Fori(1, B) as b:
                body(b, False)

        V_BANKS = (2, 7)

        def prep_dve(dve, a):
            S = prep[a]
            per = [4, 15][a]
            dve.wait_ge(weights_loaded[a], LOADED[a])
            dve.wait_ge(cleared, 1)
            nc.vector.tensor_scalar(bqs_s[a][:, :], bq_s[a][:, :], SCALE, None, ALU.mult
                                    ).then_inc(S["bqs_ready"], 1)

            def start(b, first):
                ch = Chain(dve, S["chain"], b * per)
                if a == 1:
                    dve.wait_ge(S["ol_psum"], b + 1)
                    divide(ch, 0, 5, S["o_ready"])
                    dve.wait_ge(S["o_ready"], b + 1)
                    norm_stats(dve, ch, tile(div), S, 3 * b + 1)
                    normalise(div, tile(div)).then_inc(S["ln_ready"], 1)
                    if not first:
                        finish(b - 1)
                        dve.wait_ge(S["x_kept"], b)
                    dve.wait_ge(S["y_psum"], b + 1)
                    ch.link(nc.vector.tensor_tensor(tiles(nat2), banks(5), wide(bo_s[0]), ALU.add))
                    norm_stats(dve, ch, tile(nat2), S, 3 * b + 2)
                    ch.link(normalise(nat2, tile(nat2)))
                    nc.vector.tensor_tensor(nat2[:, :], X[:, b, :], nat2[:, :], ALU.add).then_inc(S["x_ready"], 1)
                    dve.wait_ge(S["x_ready"], b + 1)
                    norm_stats(dve, ch, tile(nat2), S, 3 * b + 3)
                else:
                    dve.wait_ge(x_loaded[0] if first else x_loaded[1], 16 if first else 16 * (B - 1))
                    norm_stats(dve, ch, tile(X[:, b, :]), S, b + 1)
                if a == 1 and not first:
                    dve.wait_ge(S["xh_kept"], b)
                if not first:
                    dve.wait_ge(S["xt_psum"], b)
                normalise(nat, tile(X[:, b, :] if a == 0 else nat2)).then_inc(S["xh_ready"], 1)
                if a == 0 and not first:
                    finish(b - 1)
                assert ch.n == per, ch.n

            def finish(b):
                q, (q0, q1, q2) = qf[0][:, :], [x[:, :] for x in parts[0]]
                dve.wait_ge(S["q_rounded"], 2 * b + 1)
                nc.vector.tensor_tensor(q, q, q0, ALU.subtract).then_inc(S["q_rest"], 1)
                dve.wait_ge(S["v_psum"], b + 1)
                if not (isinstance(b, int) and b == 0):
                    dve.wait_ge(S["vst_stored"], b * (16 * UPB))
                for c in range(2):
                    ins = nc.vector.tensor_tensor(
                        vsb[:, 4 * c:4 * c + 4, :, 0:HD],
                        PS[:, V_BANKS[c], :].rearrange("p (t h d) -> p t h d", t=4, d=HD),
                        bv_s[a][:, :].rearrange("p (a h d) -> p a h d", a=1, d=HD).to_broadcast([P, 4, H, HD]),
                        ALU.add)
                ins.then_inc(S["v_ready"], 1)
                dve.wait_ge(S["q_rounded"], 2 * b + 2)
                nc.vector.tensor_tensor(q2, q, q1, ALU.subtract).then_inc(S["q_parts"], 1)

            batches(dve, start)
            finish(B - 1)
            if a == 1:
                dve.wait_ge(S["x_kept"], B)
                dve.wait_ge(S["xh_kept"], B)

        def prep_act(act, a):
            S = prep[a]
            act.wait_ge(weights_loaded[a], LOADED[a])
            act.wait_ge(S["bqs_ready"], 1)

            def start(b, first):
                if a == 1:
                    root(act, S, 3 * b + 1)
                    act.wait_ge(S["ln_psum"], b + 1)
                    for c in range(2):
                        ins = nc.scalar.activation(xT[:, c * CH:(c + 1) * CH], PS[:, 3 + c, :], ACT.Identity,
                                                   scale=lng_s[:, :], bias=lnb_s[:, :])
                    ins.then_inc(S["lnt_ready"], 1)
                    if not first:
                        finish(b - 1)
                    root(act, S, 3 * b + 2)
                    act.wait_ge(S["x_ready"], b + 1)
                    nc.scalar.copy(X[:, b, :], nat2[:, :]).then_inc(S["x_kept"], 1)
                    root(act, S, 3 * b + 3)
                else:
                    root(act, S, b + 1)
                    if not first:
                        finish(b - 1)
                act.wait_ge(S["xt_psum"], b + 1)
                for c in range(2):
                    ins = nc.scalar.copy(xT[:, c * CH:(c + 1) * CH], PS[:, 3 + c, :])
                ins.then_inc(S["xt_ready"], 1)
                if a == 1:
                    nc.scalar.copy(XH[:, b, :], nat[:, :]).then_inc(S["xh_kept"], 1)
                act.wait_ge(S["q_psum"], b + 1)
                if not first:
                    act.wait_ge(S["q_parts"], b)
                nc.scalar.activation(qf[0][:, :], PS[:, 5:7, :], ACT.Identity, scale=SCALE,
                                     bias=bqs_s[a][:, :]).then_inc(S["q_taken"], 1)
                act.wait_ge(S["k_psum"], b + 1)
                if not first:
                    act.wait_ge(S["k_parts"], b)
                nc.scalar.activation(qf[1][:, :], PS[:, 3:5, :], ACT.Identity,
                                     bias=bk_s[a][:, :]).then_inc(S["k_taken"], 1)
                if not first:
                    act.wait_ge(S["qst_stored"], b * (16 * NB))
                    act.wait_ge(S["kst_stored"], b * (16 * NB))
                act.wait_ge(S["q_taken"], b + 1)
                nc.scalar.copy(parts[0][0][:, :], qf[0][:, :]).then_inc(S["q_rounded"], 1)
                act.wait_ge(S["k_taken"], b + 1)
                nc.scalar.copy(parts[1][0][:, :], qf[1][:, :]).then_inc(S["k_rounded"], 1)

            def finish(b):
                act.wait_ge(S["q_rest"], b + 1)
                nc.scalar.copy(parts[0][1][:, :], qf[0][:, :]).then_inc(S["q_rounded"], 1)
                act.wait_ge(S["k_rest"], b + 1)
                nc.scalar.copy(parts[1][1][:, :], qf[1][:, :]).then_inc(S["k_rounded"], 1)

            batches(act, start)
            finish(B - 1)

        def prep_pe(pe, a):
            S = prep[a]
            pe.wait_ge(weights_loaded[a], LOADED[a])

            def start(b, first):
                if a == 1:
                    pe.wait_ge(S["ol_loaded"], 32 * (b + 1))
                    if not first:
                        pe.wait_ge(S["q_taken"], b)
                    transpose_outputs(0, 5).then_inc(S["ol_psum"], 1)
                    pe.wait_ge(S["ln_ready"], b + 1)
                    if not first:
                        pe.wait_ge(S["k_taken"], b)
                    transpose_tiles(3, div).then_inc(S["ln_psum"], 1)
                    pe.wait_ge(S["lnt_ready"], b + 1)
                    for t in range(NT):
                        ins = nc.tensor.matmul(PS[:, 5 + t // 4, (t % 4) * D:(t % 4 + 1) * D],
                                               xT[:, t * P:(t + 1) * P], wo_s[0][:, :], start=True, stop=True)
                    ins.then_inc(S["y_psum"], 1)
                pe.wait_ge(S["xh_ready"], b + 1)
                if not first:
                    pe.wait_ge(S["k_taken"], b)
                transpose_tiles(3, nat).then_inc(S["xt_psum"], 1)
                pe.wait_ge(S["xt_ready"], b + 1)
                if not first:
                    pe.wait_ge(S["q_taken"], b)
                for bank, w, signal in ((5, wq_s[a], S["q_psum"]), (3, wk_s[a], S["k_psum"])):
                    for c in range(2):
                        ins = nc.tensor.matmul(PS[:, bank + c, :], w[:, :], xT[:, c * CH:(c + 1) * CH],
                                               start=True, stop=True)
                    ins.then_inc(signal, 1)
                if not first:
                    pe.wait_ge(S["v_ready"], b)
                for t in range(NT):
                    ins = nc.tensor.matmul(PS[:, V_BANKS[t // 4], (t % 4) * D:(t % 4 + 1) * D],
                                           xT[:, t * P:(t + 1) * P], wv_s[a][:, :], start=True, stop=True)
                ins.then_inc(S["v_psum"], 1)

            batches(pe, start)

        def prep_pool(pool, a):
            S = prep[a]
            with pool.Fori(0, B) as b:
                k, (k0, k1, k2) = qf[1][:, :], [x[:, :] for x in parts[1]]
                pool.wait_ge(S["k_rounded"], 2 * b + 1)
                nc.gpsimd.tensor_tensor(k, k, k0, ALU.subtract).then_inc(S["k_rest"], 1)
                pool.wait_ge(S["k_rounded"], 2 * b + 2)
                nc.gpsimd.tensor_tensor(k2, k, k1, ALU.subtract).then_inc(S["k_parts"], 1)

        def prep_sp(sp, a):
            S = prep[a]

            def start(b, first):
                if a == 1:
                    if not first:
                        sp.wait_ge(S["ol_psum"], b)
                    load_outputs(sp, S["ol_loaded"], 0, b)
                if not first:
                    store(b - 1)

            def store(b):
                for st, which, pt, signal, ready in (
                        (q_st[a], QPARTS, parts[0], S["qst_stored"], S["q_parts"]),
                        (k_st[a], KPARTS, parts[1], S["kst_stored"], S["k_parts"])):
                    sp.wait_ge(ready, b + 1)
                    view = st.rearrange("(b u) j c d n -> b c (u j) d n", u=UPB)[b]
                    for c in range(NB):
                        sp.dma_start(view[c], pt[which[c]][:, :]).then_inc(signal, 16)
                sp.wait_ge(S["v_ready"], b + 1)
                view = v_st[a].rearrange("(b u) (t p) w -> b u p t w", u=UPB, p=P)[b]
                for u in range(UPB):
                    sp.dma_start(view[u], vsb[:, :, HG * u:HG * u + HG, :].rearrange("p t h d -> p t (h d)")
                                 ).then_inc(S["vst_stored"], 16)

            batches(sp, start)
            store(B - 1)
            sp.wait_ge(S["qst_stored"], B * 16 * NB)
            sp.wait_ge(S["kst_stored"], B * 16 * NB)
            sp.wait_ge(S["vst_stored"], B * 16 * UPB)

        CHAIN = 4

        def pairwise(eng, body):
            for i in (0,):
                for p in range(2):
                    body(2 * i + p, p, i)
            with eng.Fori(1, UNITS // 2 - 1) as i:
                for p in range(2):
                    body(2 * i + p, p, i)
            for i in (UNITS // 2 - 1,):
                for p in range(2):
                    body(2 * i + p, p, i)

        def ahead(v, p, i, d):
            return v + d, (p + d) % 2, i + (p + d) // 2

        def att_pe(pe, a):
            S, pl = att[a], plans[a]

            def row_scores(v, vp, vi, r):
                qt, half, width, g, hp = pl.rows[r]
                if r == 0:
                    pe.wait_ge(S["row_loaded"][vp], 64 * (vi + 1))
                x = pl.slot_of(r)
                wait(pe, S["row_read"], pl.before(v, x))
                bank = RB + x % RING
                diagonal = pl.causal and qt // 4 == half
                ins = nc.tensor.matmul(PS[:, bank, 0:width], QR[vp][hp][:, g, qt * P:(qt + 1) * P],
                                       KR[vp][:, g, half * CH:half * CH + width],
                                       start=True, stop=not diagonal)
                if diagonal:
                    ins = nc.tensor.matmul(PS[:, bank, width - P:width], identb[:, :], mask_q[:, :],
                                           start=False, stop=True)
                ins.then_inc(S["row_ready"], 1)

            def transpose_maxima(v, vp, stream):
                pe.wait_ge(S["max_ready"], v + 1)
                wait(pe, S["row_read"], pl.before(stream, TSLOT))
                bank = PS[:, RB + TSLOT % RING, :].bitcast(BF16)
                for qt in range(NT):
                    ins = nc.tensor.transpose(bank[0:4 * MROWS, qt * P:(qt + 1) * P],
                                              mparts[vp][:, qt, :, :, :].rearrange("p r m g -> p (r m g)"),
                                              identb[:, :])
                ins.then_inc(S["row_ready"], 1)

            def scores(u, p, i, s, g):
                c, kt = pl.steps[s]
                off = pl.off(c, kt)
                done, signal = (S["exp_a"], S["scores_a"]) if g == 0 else (S["exp_b"], S["scores_b"])
                if s == 0 and g == 0:
                    pe.wait_ge(S["main_loaded"][p], 80 * (i + 1))
                    pe.wait_ge(S["maxrow_loaded"][p], 16 * 2 * MROWS * (i + 1))
                wait(pe, done, pl.n * u + s)
                diagonal = pl.causal and kt // 4 == c
                for hp in range(2):
                    ins = nc.tensor.matmul(PS[:, TB + 2 * g + hp, off:CH], KS[p][hp][:, g, kt * P:(kt + 1) * P],
                                           QS[p][:, g, c * CH + off:(c + 1) * CH],
                                           start=True, stop=not diagonal)
                if diagonal:
                    for hp in range(2):
                        ins = nc.tensor.matmul(PS[:, TB + 2 * g + hp, off:off + P], identb[:, :],
                                               mask_k[:, :], start=False, stop=True)
                ins.then_inc(signal, 1)

            def values(u, p, s, part):
                c, kt = pl.steps[s]
                lo, hi = max(pl.off(c, kt), part * CH // 2), (part + 1) * CH // 2
                if part == 0:
                    pe.wait_ge(S["exp_b"], pl.n * u + s + 1)
                    if kt == 0:
                        wait(pe, S["acc_copied"], NC * u + c)
                if lo < hi:
                    for h in range(HG):
                        ins = nc.tensor.matmul(PS[32 * h:32 * h + 32, AC, lo:hi],
                                               VS[p][:, kt, 9 * h:9 * h + 32], PR[s % PRING][:, h, lo:hi],
                                               start=kt == 0 and part == 0, stop=pl.last(s),
                                               skip_group_check=True)
                    if part == 1:
                        ins.then_inc(S["pv_done"], 1)

            def body(u, p, i):
                for s in range(pl.n):
                    more = pl.stream(u, s)
                    nxt = (u, p, i, s + 1) if s + 1 < pl.n else (*ahead(u, p, i, 1), 0)
                    run_next = not (isinstance(nxt[0], int) and nxt[0] == UNITS)
                    old = (u, p, s - 1) if s else (u - 1, 1 - p, pl.n - 1)
                    run_old = not (isinstance(old[0], int) and old[0] < 0)

                    def maxima(count):
                        for _ in range(count):
                            while more:
                                v, r = more.pop(0)
                                if r is None:
                                    transpose_maxima(v, (p + 1) % 2, v + 1)
                                else:
                                    d = 1 if s + LEAD < pl.n else 2
                                    _, vp, vi = ahead(u, p, i, d)
                                    row_scores(v, vp, vi, r)
                                    break

                    anew = pl.steps[old[2]][1] == 0
                    if run_next:
                        scores(*nxt, 0)
                    maxima(1)
                    if run_old and not anew:
                        values(*old, 0)
                    maxima(1)
                    if run_next:
                        scores(*nxt, 1)
                    maxima(1)
                    if run_old and not anew:
                        values(*old, 1)
                    maxima(1)
                    if run_old and anew:
                        values(*old, 0)
                        values(*old, 1)

            for r in range(pl.nr):
                row_scores(0, 0, 0, r)
            for r in range(TSLOT):
                row_scores(1, 1, 0, r)
            transpose_maxima(0, 0, 1)
            for r in range(TSLOT, 4 * LEAD):
                row_scores(1, 1, 0, r)
            scores(0, 0, 0, 0, 0)
            scores(0, 0, 0, 0, 1)
            pairwise(pe, body)
            for part in range(2):
                values(UNITS - 1, 1, pl.n - 1, part)

        def att_dve(dve, a):
            S, pl = att[a], plans[a]

            def row_max(v, vp, r):
                qt, half, width, g, hp = pl.rows[r]
                x = pl.slot_of(r)
                dve.wait_ge(S["row_ready"], pl.used(v, x))
                nc.vector.tensor_reduce(mx[vp][:, qt, 2 * hp + g, half:half + 1],
                                        PS[:, RB + x % RING, 0:width], AX.X, ALU.max,
                                        negate=True).then_inc(S["row_read"], 1)
                if r == pl.nr - 1:
                    parts_of_max(v, vp)

            def parts_of_max(v, vp):
                dve.wait_ge(S["row_read"], pl.used(v, pl.nr))
                ch = Chain(dve, S["chain"], v * CHAIN)
                m4 = mparts[vp]
                f = nm[:, :].rearrange("p (t r g) -> p t r g", r=2, g=2)
                f2 = nm2[:, :].rearrange("p (t r g) -> p t r g", r=2, g=2)
                ch.link(nc.vector.tensor_reduce(nm[:, :], mx[vp][:, :, :, :].rearrange("p t h k -> p (t h) k"),
                                                AX.X, ALU.min))
                ch.link(nc.vector.tensor_copy(m4[:, :, :, 0, :], f))
                ch.link(nc.vector.tensor_tensor(f2, f, m4[:, :, :, 0, :], ALU.subtract))
                ch.link(nc.vector.tensor_copy(m4[:, :, :, 1, :], f2))
                ins = nc.vector.tensor_tensor(m4[:, :, :, 2, :], f2, m4[:, :, :, 1, :], ALU.subtract)
                ins.then_inc(S["max_ready"], 1)
                dve.wait_ge(S["max_ready"], v + 1)
                assert ch.n == CHAIN

            def rows_of_max(v, vp, i_prev, stream):
                dve.wait_ge(S["row_ready"], pl.used(stream, TSLOT))
                if not (isinstance(v, int) and v < 2):
                    dve.wait_ge(S["maxrow_loaded"][vp], 16 * 2 * MROWS * i_prev)
                nc.vector.tensor_copy(mrow[vp][:, :],
                                      PS[0:4 * MROWS, RB + TSLOT % RING, :].bitcast(BF16)
                                      ).then_inc(S["row_read"], 1)

            def body(u, p, i):
                for s in range(pl.n):
                    for v, r in pl.stream(u, s):
                        if r is None:
                            _, vp, vi = ahead(u, p, i, 1)
                            rows_of_max(v, vp, vi, v + 1)
                        else:
                            d = 1 if s + LEAD < pl.n else 2
                            row_max(v, (p + d) % 2, r)

            for r in range(pl.nr):
                row_max(0, 0, r)
            for r in range(TSLOT):
                row_max(1, 1, r)
            rows_of_max(0, 0, 0, 1)
            for r in range(TSLOT, 4 * LEAD):
                row_max(1, 1, r)
            pairwise(dve, body)

        def att_act(act, a):
            S, pl = att[a], plans[a]

            def exps(u, s, g):
                c, kt = pl.steps[s]
                off = pl.off(c, kt)
                ready, signal = (S["scores_a"], S["exp_a"]) if g == 0 else (S["scores_b"], S["exp_b"])
                if g == 0:
                    wait(act, S["pv_done"], pl.n * u + s - PRING + 1)
                act.wait_ge(ready, pl.n * u + s + 1)
                nc.scalar.activation(PR[s % PRING][:, 2 * g:2 * g + 2, off:CH],
                                     PS[:, TB + 2 * g:TB + 2 * g + 2, off:CH], ACT.Exp).then_inc(signal, 1)

            def copy_outputs(u, c):
                ends = [s for s in range(pl.n) if pl.last(s)]
                act.wait_ge(S["pv_done"], pl.n * u + ends[c] + 1)
                wait(act, S["o_stored"][c], 64 * u)
                nc.scalar.copy(OS[c][:, :], PS[:, AC, :]).then_inc(S["acc_copied"], 1)

            def body(u, p, i):
                for s in range(pl.n):
                    exps(u, s, 0)
                    exps(u, s, 1)
                    if s == 1 and not (isinstance(u, int) and u == 0):
                        copy_outputs(u - 1, NC - 1)
                    if s > 1 and pl.last(s - 2):
                        copy_outputs(u, pl.steps[s - 2][0])

            pairwise(act, body)
            copy_outputs(UNITS - 1, NC - 1)

        def att_sp(sp, a):
            S, pl = att[a], plans[a]

            def load_stacks(u, q_dst, k_dst, signal):
                for st, dst in ((q_st[a], q_dst), (k_st[a], k_dst)):
                    for hp in range(2):
                        buf = dst[hp] if isinstance(dst, list) else dst
                        sp.dma_start(buf[64 * hp:64 * hp + ROWS, :, :],
                                     st.rearrange("u (g r) c d n -> u r (c d) g n", r=2)[u][hp]
                                     ).then_inc(signal, 16)

            def load_main(u, p):
                load_stacks(u, QS[p], KS[p], S["main_loaded"][p])
                sp.dma_start(VS[p][:, :, 0:VW], v_st[a].rearrange("u (t p) w -> u p t w", p=P)[u]
                             ).then_inc(S["main_loaded"][p], 16)

            def load_row(u, p):
                load_stacks(u, QR[p], KR[p], S["row_loaded"][p])

            def load_maxima(u, p):
                sp.wait_ge(S["row_read"], pl.used(u + 1, TSLOT))
                for hp in range(2):
                    for m in range(MROWS):
                        row = 2 * MROWS * hp + 2 * m
                        sp.dma_start(QS[p][64 * hp + ROWS + m:64 * hp + ROWS + m + 1, :, :],
                                     mrow[p][row:row + 2, :]).then_inc(S["maxrow_loaded"][p], 16)

            def store(u, c):
                sp.wait_ge(S["acc_copied"], NC * u + c + 1)
                for h in range(HG):
                    sp.dma_start(o_st[a][u][h, :, c * CH:(c + 1) * CH], OS[c][32 * h:32 * h + HD + 1, :]
                                 ).then_inc(S["o_stored"][c], 16)

            def body(u, p, i):
                last = isinstance(u, int) and u + 1 >= UNITS
                if not last:
                    sp.wait_ge(S["scores_a"], pl.n * u + 3)
                    load_main(u + 1, 1 - p)
                if not (isinstance(u, int) and u + 2 >= UNITS):
                    sp.wait_ge(S["row_ready"], pl.used(u, pl.nr))
                    load_row(u + 2, p)
                store(u, 0)
                if not last:
                    load_maxima(u + 1, 1 - p)
                store(u, 1)

            load_row(0, 0)
            load_main(0, 0)
            load_row(1, 1)
            load_maxima(0, 0)
            pairwise(sp, body)
            for c in range(NC):
                sp.wait_ge(S["o_stored"][c], 64 * UNITS)

        SLOTS = NC * E
        WORK, SMALL = 5, 7

        def pieces(eng, b, before, experts, after):
            for n in range(SLOTS):
                experts(n)
                if b + 1 < B:
                    before(b + 1, n)
                if b > 0:
                    after(b - 1, n)

        def tail_sp(sp):
            S = tail

            def store(b):
                sp.wait_ge(S["out_ready"], b + 1)
                sp.dma_start(out_d.rearrange("b (t p) d -> b p t d", p=P)[b], tiles(res)
                             ).then_inc(S["out_stored"], 16)

            for b in range(B):
                wait(sp, S["ol_psum"], b)
                load_outputs(sp, S["ol_loaded"], 1, b)
            for b in range(B):
                store(b)
            sp.wait_ge(S["out_stored"], 16 * B)

        def tail_dve(dve):
            S, V = tail, nc.vector
            ch = Chain(dve, S["chain"], 0)
            rows = lambda v: v[:, :].rearrange("p (t a) -> p t a", a=1).to_broadcast([P, NT, E])
            roots = [0]

            def ask_root(src):
                variance(ch, src, S)
                roots[0] += 1

            def before(b, n):
                x = xf[b % 2]
                if n == 0:
                    dve.wait_ge(S["ol_psum"], b + 1)
                    divide(ch, WORK, SMALL, S["o_ready"])
                elif n == 2:
                    dve.wait_ge(S["y_psum"], b + 1)
                    ch.link(V.tensor_tensor(tiles(x), banks(WORK), wide(bo_s[1]), ALU.add))
                    ch.link(V.tensor_tensor(x[:, :], x[:, :], XH[:, b, :], ALU.add))
                elif n == 3:
                    ask_root(tile(x))
                elif n == 4:
                    deviation(dve, ch, S, roots[0])
                    ch.link(normalise(x, tile(x)))
                    ch.link(V.tensor_tensor(tiles(x), tiles(x), wide(l1g_s), ALU.mult))
                elif n == 5:
                    V.tensor_tensor(tiles(x), tiles(x), wide(l1b_s), ALU.add).then_inc(S["xf_ready"], 1)
                    dve.wait_ge(S["xf_ready"], b + 1)
                elif n == 7:
                    dve.wait_ge(S["logit_psum"], b + 1)
                    ch.link(V.tensor_tensor(lg[:, :, :], PS[:, SMALL, 0:NT * E].rearrange("p (t e) -> p t e", e=E),
                                            gb_s[:, :].rearrange("p (a e) -> p a e", a=1).to_broadcast([P, NT, E]),
                                            ALU.add))
                    ch.link(V.reduce_max(gs[:, :], lg[:, :, :], AX.X))
                    V.tensor_tensor(lg[:, :, :], lg[:, :, :], rows(gs), ALU.subtract).then_inc(S["shifted"], 1)
                elif n == 8:
                    dve.wait_ge(S["exp_ready"], b + 1)
                    ch.link(V.reduce_sum(gs[:, :], ge[:, :, :], AX.X))
                    ch.link(V.reciprocal(gs[:, :], gs[:, :]))
                    ch.link(V.tensor_tensor(ge[:, :, :], ge[:, :, :], rows(gs), ALU.mult))
                this = ge[:, :, :].rearrange("p t (e a) -> p t e a", a=1).to_broadcast([P, NT, E, E])
                other = ge[:, :, :].rearrange("p t (a e) -> p t a e", a=1).to_broadcast([P, NT, E, E])
                earlier = before_e[:, :, :].rearrange("p (a e) f -> p a e f", a=1).to_broadcast([P, NT, E, E])
                if n == 8:
                    ch.link(V.tensor_tensor(cmp1[:, :, :, :], other, this, ALU.is_gt))
                elif n == 9:
                    ch.link(V.tensor_tensor(cmp2[:, :, :, :], other, this, ALU.is_equal))
                    ch.link(V.tensor_tensor(cmp2[:, :, :, :], cmp2[:, :, :, :], earlier, ALU.mult))
                    ch.link(V.tensor_tensor(cmp1[:, :, :, :], cmp1[:, :, :, :], cmp2[:, :, :, :], ALU.add))
                elif n == 10:
                    ch.link(V.reduce_sum(lg[:, :, :], cmp1[:, :, :, :], AX.X))
                    V.scalar_tensor_tensor(wt[b % 2][:, :, :], lg[:, :, :], 2.0, ge[:, :, :], ALU.is_lt,
                                           ALU.mult).then_inc(S["wt_ready"], 1)
                    dve.wait_ge(S["wt_ready"], b + 1)

            def experts(b):
                def add(n):
                    c, e = n // E, n % E
                    y = acc[b % 2]
                    if e == 0:
                        part = slice(c * CH, (c + 1) * CH)
                        dve.wait_ge(S["bias_psum"], NC * b + c + 1)
                        V.tensor_tensor(y[:, part], xf[b % 2][:, part], PS[:, 4, :], ALU.add
                                        ).then_inc(S["acc_begun"], 1)
                        dve.wait_ge(S["acc_begun"], NC * b + c + 1)
                    else:
                        dve.wait_ge(S["e_added"], SLOTS * b + n)
                    dve.wait_ge(S["e_psum"], SLOTS * b + n + 1)
                    for t in range(4):
                        tt = 4 * c + t
                        yt = y[:, tt * D:(tt + 1) * D]
                        ins = V.scalar_tensor_tensor(yt, PS[:, 2 + n % 2, t * D:(t + 1) * D],
                                                     wt[b % 2][:, tt, e:e + 1], yt, ALU.mult, ALU.add)
                    ins.then_inc(S["e_added"], 1)
                return add

            def after(b, n):
                y = acc[b % 2]
                if n == 11:
                    dve.wait_ge(S["e_added"], SLOTS * (b + 1))
                    ask_root(tile(y))
                elif n == 12:
                    deviation(dve, ch, S, roots[0])
                    ch.link(normalise(y, tile(y)))
                elif n == 13:
                    ch.link(V.tensor_tensor(spread(y), spread(y), wide(l2g_s), ALU.mult))
                    ch.link(V.tensor_tensor(spread(y), spread(y), wide(l2b_s), ALU.add))
                elif n == 14:
                    ask_root(tile(y))
                elif n == 15:
                    deviation(dve, ch, S, roots[0])
                    ch.link(normalise(y, tile(y)))
                    wait(dve, S["out_stored"], 16 * b)
                    V.tensor_tensor(res[:, :], y[:, :], X[:, b, :], ALU.add).then_inc(S["out_ready"], 1)
                    dve.wait_ge(S["out_ready"], b + 1)

            for n in range(SLOTS):
                before(0, n)
            for b in range(B):
                pieces(dve, b, before, experts(b), after)
            for n in range(SLOTS):
                after(B - 1, n)

        def tail_act(act):
            S = tail
            roots = [0]

            def next_root():
                roots[0] += 1
                root(act, S, roots[0])

            def take(dst, src, signal):
                nc.scalar.copy(dst, src).then_inc(signal, 1)

            def before(b, n):
                if n == 1:
                    act.wait_ge(S["on_psum"], b + 1)
                    take(oN, PS[:, WORK:WORK + 2, :].rearrange("p c n -> p (c n)"), S["on_ready"])
                elif n == 4:
                    next_root()
                elif n == 6:
                    act.wait_ge(S["xf_psum"], b + 1)
                    take(xTs[b % 2], PS[:, WORK:WORK + 2, :].rearrange("p c n -> p (c n)"), S["xt_ready"])
                elif n == 8:
                    act.wait_ge(S["shifted"], b + 1)
                    nc.scalar.activation(ge[:, :, :], lg[:, :, :], ACT.Exp).then_inc(S["exp_ready"], 1)
                elif n == 11:
                    act.wait_ge(S["wt_psum"], b + 1)
                    take(wT, PS[0:E, WORK:WORK + 2, :].rearrange("p c n -> p (c n)"), S["wT_ready"])

            def relus(m):
                e = m % E
                for f in range(2):
                    act.wait_ge(S["h_psum"], 2 * m + f + 1)
                    nc.scalar.activation(hT[m % 2][:, f, :], PS[:, f, :], ACT.Relu,
                                         bias=b1_s[:, e, f:f + 1]).then_inc(S["h_ready"], 1)

            def experts(b):
                def next_relus(n):
                    if SLOTS * b + n + 1 < SLOTS * B:
                        relus(SLOTS * b + n + 1)
                return next_relus

            def after(b, n):
                if n in (12, 15):
                    next_root()

            for n in range(SLOTS):
                before(0, n)
            relus(0)
            for b in range(B):
                pieces(act, b, before, experts(b), after)
            for n in range(SLOTS):
                after(B - 1, n)

        def tail_pe(pe):
            S = tail

            def before(b, n):
                if n == 0:
                    pe.wait_ge(S["ol_loaded"], 32 * (b + 1))
                    wait(pe, S["wT_ready"], b)
                    transpose_outputs(WORK, SMALL).then_inc(S["ol_psum"], 1)
                elif n == 1:
                    pe.wait_ge(S["o_ready"], b + 1)
                    transpose_tiles(WORK, div).then_inc(S["on_psum"], 1)
                elif n == 2:
                    pe.wait_ge(S["on_ready"], b + 1)
                    for t in range(NT):
                        ins = nc.tensor.matmul(PS[:, WORK + t // 4, (t % 4) * D:(t % 4 + 1) * D],
                                               oN[:, t * P:(t + 1) * P], wo_s[1][:, :], start=True, stop=True)
                    ins.then_inc(S["y_psum"], 1)
                elif n == 6:
                    pe.wait_ge(S["xf_ready"], b + 1)
                    transpose_tiles(WORK, xf[b % 2]).then_inc(S["xf_psum"], 1)
                elif n == 7:
                    pe.wait_ge(S["xt_ready"], b + 1)
                    for t in range(NT):
                        ins = nc.tensor.matmul(PS[:, SMALL, t * E:(t + 1) * E], xTs[b % 2][:, t * P:(t + 1) * P],
                                               gw_s[:, :], start=True, stop=True)
                    ins.then_inc(S["logit_psum"], 1)
                elif n == 11:
                    pe.wait_ge(S["wt_ready"], b + 1)
                    for t in range(NT):
                        ins = nc.tensor.transpose(PS[0:E, WORK + t // 4, (t % 4) * P:(t % 4 + 1) * P],
                                                  wt[b % 2][:, t, :], ident[:, :])
                    ins.then_inc(S["wt_psum"], 1)

            def hidden(m):
                b, c, e = m // SLOTS, m % SLOTS // E, m % E
                if m == 0 or m % SLOTS == 0:
                    pe.wait_ge(S["xt_ready"], b + 1)
                for f in range(2):
                    wait(pe, S["h_ready"], 2 * (m - 1) + f + 1)
                    nc.tensor.matmul(PS[:, f, :], w1_s[:, e, f * P:(f + 1) * P],
                                     xTs[b % 2][:, c * CH:(c + 1) * CH], start=True, stop=True
                                     ).then_inc(S["h_psum"], 1)

            def second(m):
                e = m % E
                pe.wait_ge(S["h_ready"], 2 * m + 2)
                wait(pe, S["e_added"], m - 1)
                for t in range(4):
                    for f in range(2):
                        ins = nc.tensor.matmul(PS[:, 2 + m % 2, t * D:(t + 1) * D],
                                               hT[m % 2][:, f, t * P:(t + 1) * P], w2_s[:, e, f, :],
                                               start=f == 0, stop=f == 1)
                ins.then_inc(S["e_psum"], 1)

            def bias(b, c):
                pe.wait_ge(S["wT_ready"], b + 1)
                wait(pe, S["acc_begun"], NC * b + c)
                for t in range(4):
                    tt = 4 * c + t
                    ins = nc.tensor.matmul(PS[:, 4, t * D:(t + 1) * D], wT[:, tt * P:(tt + 1) * P],
                                           b2_s[:, :], start=True, stop=True)
                ins.then_inc(S["bias_psum"], 1)

            def experts(b):
                def expert(n):
                    m = SLOTS * b + n
                    if n % E == 0:
                        bias(b, n // E)
                    if m + 1 < SLOTS * B:
                        hidden(m + 1)
                    second(m)
                return expert

            for n in range(SLOTS):
                before(0, n)
            hidden(0)
            for b in range(B):
                pieces(pe, b, before, experts(b), lambda b, n: None)

        @block.sync
        def _(sp):
            sp.dma_start(spread(X[:, 0, :]), x_view[0]).then_inc(x_loaded[0], 16)
            for dst, src in loads[0]:
                sp.dma_start(dst, src, allow_slow_non_contiguous=True).then_inc(weights_loaded[0], 16)
            for b in range(1, B):
                sp.dma_start(spread(X[:, b, :]), x_view[b]).then_inc(x_loaded[1], 16)
            for dst, src in loads[1]:
                sp.dma_start(dst, src, allow_slow_non_contiguous=True).then_inc(weights_loaded[1], 16)
            prep_sp(sp, 0)
            sp.wait_ge(cleared, CLEARED)
            att_sp(sp, 0)
            prep_sp(sp, 1)
            att_sp(sp, 1)
            tail_sp(sp)

        @block.vector
        def _(dve):
            for p in range(2):
                nc.vector.memset(mx[p][:, :, :, :], 3e38)
            nc.vector.memset(before_e[:, :, :], 0.0).then_inc(const_dve, 1)
            dve.wait_ge(const_dve, 1)
            for e in range(1, E):
                ins = nc.vector.memset(before_e[:, e, 0:e], 1.0)
            ins.then_inc(const_dve, 1)
            dve.wait_ge(const_dve, 2)
            prep_dve(dve, 0)
            att_dve(dve, 0)
            prep_dve(dve, 1)
            att_dve(dve, 1)
            tail_dve(dve)

        @block.scalar
        def _(act):
            prep_act(act, 0)
            att_act(act, 0)
            prep_act(act, 1)
            att_act(act, 1)
            tail_act(act)

        @block.gpsimd
        def _(pool):
            nc.gpsimd.memset(ident[:, :], 0.0)
            nc.gpsimd.memset(mask_q[:, :], 0.0)
            nc.gpsimd.memset(mask_k[:, :], 0.0).then_inc(const_ready, 1)
            pool.wait_ge(const_ready, 1)
            nc.gpsimd.affine_select(out=ident[:, :], in_=ident[:, :], compare_op=ALU.not_equal, fill=1.0,
                                    base=0, pattern=[[-1, P]], channel_multiplier=1)
            nc.gpsimd.affine_select(out=mask_q[:, :], in_=mask_q[:, :], compare_op=ALU.is_ge, fill=NEG,
                                    base=0, pattern=[[-1, P]], channel_multiplier=1)
            nc.gpsimd.affine_select(out=mask_k[:, :], in_=mask_k[:, :], compare_op=ALU.is_ge, fill=NEG,
                                    base=0, pattern=[[1, P]], channel_multiplier=-1).then_inc(const_ready, 1)
            pool.wait_ge(const_ready, 2)
            nc.gpsimd.tensor_copy(identb[:, :], ident[:, :]).then_inc(const_ready, 1)
            nc.gpsimd.memset(vsb[:, :, :, :], 1.0).then_inc(cleared, 1)
            for buf in (*KS[0], *KS[1], *QR[0], *QR[1], *QS, *KR, *VS):
                ins = nc.gpsimd.memset(buf[:, :, :], 0.0)
            for h in range(2):
                ins.then_inc(cleared, 1)
                pool.wait_ge(cleared, h + 2)
                for p in range(2):
                    ins = nc.gpsimd.memset(KS[p][h][64 * h:64 * h + 64, :, :], 1.0)
            ins.then_inc(cleared, 1)
            pool.wait_ge(cleared, CLEARED)
            prep_pool(pool, 0)
            prep_pool(pool, 1)

        @block.tensor
        def _(pe):
            pe.wait_ge(const_ready, 3)
            prep_pe(pe, 0)
            att_pe(pe, 0)
            prep_pe(pe, 1)
            att_pe(pe, 1)
            tail_pe(pe)


_INS = ["L0_attn_x"] + ["L0_attn_" + n for n in "Wq bq Wk bk Wv bv ln_g ln_b Wo bo".split()] + \
       ["L0_ffn_" + n for n in "Wq bq Wk bk Wv bv Wo bo gW gb W1 b1 W2 b2 ln1_g ln1_b ln2_g ln2_b".split()]


def kernel(**inputs):
    import numpy as _np
    import concourse.bacc as _bacc
    from concourse import mybir as _mybir
    from concourse.bass_utils import run_bass_kernel_spmd as _run

    nc = _bacc.Bacc("TRN2", target_bir_lowering=False, num_devices=1)
    arrays, args = {}, []
    for name in _INS:
        a = _np.ascontiguousarray(inputs[name])
        arrays[f"in_{name}_dram"] = a
        args.append(nc.dram_tensor(f"in_{name}_dram", a.shape, _mybir.dt.from_np(a.dtype), kind="ExternalInput").ap())
    args.append(nc.dram_tensor("out_0_dram", (B, N, D), _mybir.dt.float32, kind="ExternalOutput").ap())
    sandwich(nc, *args)
    r = _run(nc, [arrays], core_ids=[0])
    return r.results[0]["out_0_dram"]
```

```python
import concourse.bass as bass
from concourse import mybir
from contextlib import ExitStack

FP32 = mybir.dt.float32
BF16 = mybir.dt.bfloat16
ALU = mybir.AluOpType
ACT = mybir.ActivationFunctionType
AX = mybir.AxisListType

B, N, D = 4, 1024, 128
P = 128
H, HD = 16, 8
E, FF = 8, 256
NT = N // P
HG = 4
UNITS = B * H // HG
UPB = H // HG
CH = 512
NC = N // CH
QPARTS = [0, 0, 0, 1, 1, 2]
KPARTS = [0, 1, 2, 0, 1, 0]
NB = len(QPARTS)
ROWS = NB * HD
MROWS = 3
VW = HG * (HD + 1)
VPAD = 60
SCALE = float(HD) ** -0.5
EPS = 1e-5
NEG = -1e30
LEAD = 5
RING = 3
MEANWHILE = 8
PRING = 4
TSLOT = 4


def wait(eng, sem, value):
    if isinstance(value, int) and value <= 0:
        return
    eng.wait_ge(sem, value)


class Plan:

    def __init__(self, causal):
        self.causal = causal
        self.steps = [(c, kt) for c in range(NC) for kt in range(NT)
                      if not causal or kt * P < (c + 1) * CH]
        self.n = len(self.steps)
        self.rows = []
        for qt in range(NT):
            for half in range(NC):
                width = min(CH, (qt + 1) * P - half * CH) if causal else CH
                if width > 0:
                    self.rows += [(qt, half, width, g, r) for g in range(2) for r in range(2)]
        self.nr = len(self.rows)
        self.per = self.nr // self.n
        assert self.per == 4 and self.nr == 4 * self.n
        self.used_slots = self.nr + 1
        self.slots = -(-self.used_slots // RING) * RING

    def off(self, c, kt):
        return max(0, kt * P - c * CH) if self.causal else 0

    def first(self, c, kt):
        return kt == 0

    def last(self, s):
        return s == self.n - 1 or self.steps[s + 1][0] != self.steps[s][0]

    def slot_of(self, r):
        return r if r < TSLOT else r + 1

    def used(self, v, x):
        if isinstance(v, int) and v == 0 and x < TSLOT:
            return x + 1
        if isinstance(v, int) and v == UNITS:
            return v * self.used_slots
        return v * self.used_slots + x

    def before(self, v, x):
        alone = isinstance(v, int) and v == UNITS
        if x >= RING and not alone:
            return self.used(v, x - RING)
        y = self.slots - RING + x % RING
        while y > self.nr:
            y -= RING
        if isinstance(v, int) and v == 0:
            return 0
        return self.used(v - 1, y)

    def stream(self, u, s):
        t = s + LEAD
        v, base = (u + 1, 4 * t) if t < self.n else (u + 2, 4 * (t - self.n))
        over = isinstance(v, int) and v >= UNITS
        out = []
        for r in range(base, base + 4):
            if r == TSLOT and (not isinstance(v, int) or v <= UNITS):
                out.append((v - 1, None))
            if not over:
                out.append((v, r))
        return out


def sandwich(nc, x_d, wq1, bq1, wk1, bk1, wv1, bv1, lng1, lnb1, wo1, bo1,
             wq2, bq2, wk2, bk2, wv2, bv2, wo2, bo2, gw, gb, w1, b1, w2, b2,
             l1g, l1b, l2g, l2b, out_d):
    ctx = ExitStack()

    def sb(name, shape, dt=FP32):
        return ctx.enter_context(nc.sbuf_tensor(name, shape, dt))

    def dram(name, shape, dt):
        return nc.dram_tensor(name, shape, dt, kind="Internal").ap()

    def sem(name):
        return ctx.enter_context(nc.semaphore(name))

    with ctx:
        q_st = [dram(f"q_st{a}", (UNITS, HG, NB, HD, N), BF16) for a in range(2)]
        k_st = [dram(f"k_st{a}", (UNITS, HG, NB, HD, N), BF16) for a in range(2)]
        v_st = [dram(f"v_st{a}", (UNITS, N, VW), FP32) for a in range(2)]
        o_st = [dram(f"o_st{a}", (UNITS, HG, HD + 1, N), FP32) for a in range(2)]

        wq_s = [sb(f"wq{a}", [P, D]) for a in range(2)]
        wk_s = [sb(f"wk{a}", [P, D]) for a in range(2)]
        wv_s = [sb(f"wv{a}", [P, D]) for a in range(2)]
        wo_s = [sb(f"wo{a}", [P, D]) for a in range(2)]
        bq_s = [sb(f"bq{a}", [P, 1]) for a in range(2)]
        bk_s = [sb(f"bk{a}", [P, 1]) for a in range(2)]
        bv_s = [sb(f"bv{a}", [P, D]) for a in range(2)]
        bo_s = [sb(f"bo{a}", [P, D]) for a in range(2)]
        lng_s, lnb_s = sb("lng", [P, 1]), sb("lnb", [P, 1])
        gw_s, gb_s = sb("gw", [P, E]), sb("gb", [P, E])
        w1_s, b1_s = sb("w1", [P, E, FF]), sb("b1", [P, E, 2])
        w2_s, b2_s = sb("w2", [P, E, 2, D]), sb("b2", [E, D])
        l1g_s, l1b_s = sb("l1g", [P, D]), sb("l1b", [P, D])
        l2g_s, l2b_s = sb("l2g", [P, D]), sb("l2b", [P, D])
        ident = sb("ident", [P, P])
        identb = sb("identb", [P, P], BF16)
        mask_q = sb("mask_q", [P, P], BF16)
        mask_k = sb("mask_k", [P, P], BF16)
        before_e = sb("before_e", [P, E, E])

        X = sb("X", [P, B, NT * D])
        XH = sb("XH", [P, B, NT * D])
        xT = sb("xT", [P, N])
        nat = sb("nat", [P, NT * D])
        nat2 = sb("nat2", [P, NT * D])
        bnst, dif = sb("bnst", [P, NT, 6]), sb("dif", [P, NT])
        mean, std, rstd = ([sb(f"{name}{k}", [P, NT]) for k in range(2)] for name in ("mean", "std", "rstd"))
        vsb = sb("vsb", [P, NT, H, HD + 1])
        oT, lT, rl = sb("oT", [P, N]), sb("lT", [H, N]), sb("rl", [P, NT * H])
        bqs_s = [sb(f"bqs{a}", [P, 1]) for a in range(2)]
        res, div = sb("res", [P, NT * D]), sb("div", [P, NT * D])
        QS = [sb(f"QS{p}", [P, 2, N], BF16) for p in range(2)]
        KS = [[sb(f"KS{p}{h}", [P, 2, N], BF16) for h in range(2)] for p in range(2)]
        QR = [[sb(f"QR{p}{h}", [P, 2, N], BF16) for h in range(2)] for p in range(2)]
        KR = [sb(f"KR{p}", [P, 2, N], BF16) for p in range(2)]
        VS = [sb(f"VS{p}", [P, NT, VPAD]) for p in range(2)]
        PR = [sb(f"PR{p}", [P, HG, CH]) for p in range(PRING)]
        OS = [sb(f"OS{c}", [P, CH]) for c in range(NC)]
        mx = [sb(f"mx{p}", [P, NT, 4, 2]) for p in range(2)]
        nm, nm2 = sb("nm", [P, NT * 4]), sb("nm2", [P, NT * 4])
        mparts = [sb(f"mparts{p}", [P, NT, 2, MROWS, 2], BF16) for p in range(2)]
        mrow = [sb(f"mrow{p}", [4 * MROWS, N], BF16) for p in range(2)]
        flat = lambda buf, k: buf[:, 2 * k:2 * k + 2, :].rearrange("p a n -> p (a n)")
        norm = [nat[:, :], flat(PR[0], 0)]
        work = [nat2[:, :], flat(PR[0], 1)]
        featT = [xT[:, :], flat(PR[1], 0)]
        qf = [[sb(f"{name}f", [P, N])[:, :], other] for name, other in
              (("q", flat(PR[1], 1)), ("k", flat(PR[2], 0)))]
        parts = [[[sb(f"part{t}{j}", [P, N], BF16)[:, :] for j in range(3)] for t in range(2)],
                 [[part[:, 2 * k:2 * k + 2, :].rearrange("p a n -> p (a n)").bitcast(BF16)[:, i * N:(i + 1) * N]
                   for part, k, i in row] for row in
                  (((PR[2], 1, 0), (PR[2], 1, 1), (PR[3], 0, 0)), ((PR[3], 0, 1), (PR[3], 1, 0), (PR[3], 1, 1)))]]
        lg, ge = sb("lg", [P, NT, E]), sb("ge", [P, NT, E])
        wt = [sb(f"wt{p}", [P, NT, E]) for p in range(2)]
        gs = sb("gs", [P, NT])
        acc = [flat(PR[0], k) for k in range(2)]
        hT = [PR[1][:, 2 * k:2 * k + 2, :] for k in range(2)]
        cmp1, cmp2 = (qf[1][0][:, k * CH:(k + 1) * CH].rearrange("p (t e f) -> p t e f", t=NT, e=E)
                      for k in range(2))
        oN = [nat2[:, :], *[flat(PR[2], 1)] * (B - 1)]
        xTs = [xT[:, :], flat(PR[3], 0)]
        wT = qf[0][0][0:E, :]
        xf = [nat, nat2]

        PS = ctx.enter_context(nc.psum_tensor("PS", [P, 8, CH], FP32))
        TB = 0
        AC = 4
        RB = 5

        x_loaded = [sem("x_first_loaded"), sem("x_rest_loaded")]
        weights_loaded = [sem(f"weights{a}_loaded") for a in range(2)]
        const_ready = sem("const_ready")
        const_dve = sem("const_dve")
        cleared, CLEARED = sem("cleared"), 4
        block = ctx.enter_context(nc.Block())

        x_view = x_d.rearrange("b (t p) d -> b p t d", p=P)
        loads = [[], []]
        col = lambda v: v.rearrange("(p a) -> p a", a=1)
        bc = lambda v, n: v.rearrange("(a n) -> a n", a=1).to_broadcast([P, n])
        for a, (wq, wk, wv, bq, bk, bv) in enumerate([(wq1, wk1, wv1, bq1, bk1, bv1),
                                                      (wq2, wk2, wv2, bq2, bk2, bv2)]):
            loads[a] += [(wq_s[a][:, :], wq), (bq_s[a][:, :], col(bq))]
            kv = wk.shape[1]
            for c in range(0, D, kv):
                loads[a] += [(wk_s[a][:, c:c + kv], wk), (bk_s[a][c:c + kv, :], col(bk)),
                             (wv_s[a][:, c:c + kv], wv), (bv_s[a][:, c:c + kv], bc(bv, kv))]
        loads[1] += [(wo_s[0][:, :], wo1), (wo_s[1][:, :], wo2), (bo_s[0][:, :], bc(bo1, D)),
                     (bo_s[1][:, :], bc(bo2, D)), (lng_s[:, :], col(lng1)), (lnb_s[:, :], col(lnb1)),
                     (gw_s[:, :], gw), (gb_s[:, :], bc(gb, E)), (b2_s[:, :], b2),
                     (w1_s[:, :, :], w1.rearrange("e d f -> d e f"))]
        for e in range(E):
            loads[1] += [(b1_s[:, e, :], b1[e].rearrange("(a f) -> f a", a=2)),
                         (w2_s[:, e, :, :], w2[e].rearrange("(a f) d -> f a d", a=2))]
        loads[1] += [(dst[:, :], bc(src, D)) for dst, src in
                     ((l1g_s, l1g), (l1b_s, l1b), (l2g_s, l2g), (l2b_s, l2b))]
        LOADED = [16 * len(part) for part in loads]

        def signals(phase, names):
            return {name: sem(f"{phase}_{name}") for name in names.split()}

        PREP = ("chain ol_loaded ol_psum o_ready var_ready std_ready ln_ready ln_psum lnt_ready y_psum "
                "bqs_ready x_ready xh_ready xt_psum xt_ready q_psum k_psum v_psum q_taken k_taken "
                "q_first k_first q_second k_second q_rest k_rest q_parts k_parts v_ready vst_stored")
        prep = [signals(f"prep{a}", PREP) for a in range(2)]
        for a in range(2):
            for name in ("qst_stored", "kst_stored"):
                prep[a][name] = [sem(f"prep{a}_{name}{k}") for k in range(2)]
        TAIL = ("chain ol_loaded ol_psum o_ready on_psum on_ready y_psum var_ready std_ready xf_ready "
                "xf_psum xt_ready logit_psum shifted exp_ready wt_ready wt_psum wT_ready bias_psum "
                "acc_begun h_psum h_ready e_psum e_added out_ready out_stored last_ready last_stored")
        tail = signals("tail", TAIL)
        ATT = ("row_ready row_read chain max_ready scores_a scores_b exp_a exp_b pv_done "
               "acc_copied")
        att = [signals(f"att{a}", ATT) for a in range(2)]
        for a in range(2):
            for name, n in (("row_loaded", 2), ("main_loaded", 2), ("maxrow_loaded", 2), ("o_stored", NC)):
                att[a][name] = [sem(f"att{a}_{name}{p}") for p in range(n)]
        plans = [Plan(True), Plan(False)]

        class Chain:

            def __init__(self, eng, counts, base):
                self.eng, self.counts, self.base, self.n = eng, counts, base, 0

            def link(self, ins):
                self.n += 1
                ins.then_inc(self.counts, 1)
                self.eng.wait_ge(self.counts, self.base + self.n)

        class Norms:

            def __init__(self, S):
                self.S, self.n = S, 0

            def ask(self, chain, src, tiles=range(NT)):
                k = self.n % 2
                self.n += 1
                for t in tiles:
                    ins = nc.vector.bn_stats(bnst[:, t, :], src(t))
                chain.link(ins)
                of = slice(tiles.start, tiles.stop)
                mean_e, sq_e, mean_o, sq_o = (bnst[:, of, j] for j in (1, 2, 4, 5))
                m, v, d = mean[k][:, of], std[k][:, of], dif[:, of]
                nc.vector.tensor_tensor(m, mean_e, mean_o, ALU.add)
                nc.vector.tensor_tensor(d, mean_e, mean_o, ALU.subtract)
                chain.link(nc.vector.scalar_tensor_tensor(v, sq_e, D * EPS, sq_o, ALU.add, ALU.add))
                nc.vector.tensor_scalar(m, m, 0.5, None, ALU.mult)
                chain.link(nc.vector.scalar_tensor_tensor(d, d, D / 4.0, d, ALU.mult, ALU.mult))
                nc.vector.tensor_tensor(v, v, d, ALU.add).then_inc(self.S["var_ready"], 1)
                return self.n

            def root(self, act, tiles=range(NT)):
                k, of = self.n % 2, slice(tiles.start, tiles.stop)
                self.n += 1
                act.wait_ge(self.S["var_ready"], self.n)
                nc.scalar.activation(std[k][:, of], std[k][:, of], ACT.Sqrt, scale=1.0 / D
                                     ).then_inc(self.S["std_ready"], 1)

            def normalise(self, dve, chain, n, dst, src, tiles=range(NT)):
                k, of = (n - 1) % 2, slice(tiles.start, tiles.stop)
                dve.wait_ge(self.S["std_ready"], n)
                chain.link(nc.vector.reciprocal(rstd[k][:, of], std[k][:, of]))
                for t in tiles:
                    ins = nc.vector.tensor_scalar(dst[:, t * D:(t + 1) * D], src(t), mean[k][:, t:t + 1],
                                                  rstd[k][:, t:t + 1], ALU.subtract, ALU.mult)
                return ins

        def tile(buf):
            return lambda t: buf[:, t * D:(t + 1) * D]

        def wide(v, n=NT):
            return v[:, :].rearrange("p (a d) -> p a d", a=1).to_broadcast([P, n, D])

        def banks(bank):
            return PS[:, bank:bank + 2, :].rearrange("p c (t d) -> p (c t) d", d=D)

        def tiles(buf):
            return buf[:, :].rearrange("p (t d) -> p t d", d=D)

        def spread(x):
            return x.rearrange("p (t d) -> p t d", d=D)

        def divide(chain, dst, o_banks, l_bank, signal):
            chain.link(nc.vector.reciprocal(rl[:, :], PS[:, l_bank, 0:NT * H]))
            nc.vector.tensor_tensor(
                dst.rearrange("p (h d) -> p h d", d=HD),
                PS[:, o_banks:o_banks + 2, :].rearrange("p c (h d) -> p (c h) d", d=HD),
                rl[:, :].rearrange("p (h a) -> p h a", a=1).to_broadcast([P, NT * H, HD]),
                ALU.mult).then_inc(signal, 1)

        def transpose_tiles(bank, src):
            for t in range(NT):
                ins = nc.tensor.transpose(PS[:, bank + t // 4, (t % 4) * P:(t % 4 + 1) * P],
                                          src[:, t * P:(t + 1) * P], ident[:, :])
            return ins

        def transpose_outputs(o_banks, l_bank):
            transpose_tiles(o_banks, oT)
            for t in range(NT):
                ins = nc.tensor.transpose(PS[:, l_bank, t * H:(t + 1) * H], lT[:, t * P:(t + 1) * P],
                                          ident[0:H, 0:H])
            return ins

        def load_outputs(sp, signal, a, b):
            view = o_st[a].rearrange("(b u) j r n -> b (u j) r n", u=UPB)[b]
            sp.dma_start(oT[:, :], view[:, 0:HD, :]).then_inc(signal, 16)
            sp.dma_start(lT[:, :], view[:, HD, :]).then_inc(signal, 16)

        STEPS, K_BANK, V_BANK = 9, 4, 6
        BESIDE = 5

        def staggered(a, step, done=0):
            first, begin = (0, (-5, 0, 3, 6)) if a else (3, (-3, -1, 1, 3))
            for g in range(begin[B - 1] + STEPS):
                for b in (range(B - 1, -1, -1) if a else range(B)):
                    s = g - begin[b]
                    if max(first, done if b == 0 else 0) <= s < STEPS:
                        step(b, s)

        def sum_bank(b):
            return RB + 2 if b == 0 else K_BANK

        def work_bank(a, b):
            return RB if a == 1 and b == 0 else 2 * (b % 2)

        def prep_dve(dve, a):
            S, V = prep[a], nc.vector
            ch, norms, asked = Chain(dve, S["chain"], 0), Norms(S), {}

            def step(b, s):
                if (b, s) == (0, 4):
                    dve.wait_ge(cleared, 1)
                    dve.wait_ge(weights_loaded[a], LOADED[a])
                    V.tensor_scalar(bqs_s[a][:, :], bq_s[a][:, :], SCALE, None, ALU.mult
                                    ).then_inc(S["bqs_ready"], 1)
                y, q = work[b % 2], qf[0][b % 2]
                q0, q1, q2 = parts[b % 2][0]
                if s == 0:
                    dve.wait_ge(S["ol_psum"], b + 1)
                    divide(ch, y, work_bank(a, b), sum_bank(b), S["o_ready"])
                    dve.wait_ge(S["o_ready"], b + 1)
                    asked[b] = norms.ask(ch, tile(y))
                elif s == 1:
                    norms.normalise(dve, ch, asked[b], y, tile(y)).then_inc(S["ln_ready"], 1)
                elif s == 2:
                    dve.wait_ge(S["y_psum"], b + 1)
                    if b == 0:
                        dve.wait_ge(weights_loaded[a], LOADED[a])
                    ch.link(V.tensor_tensor(spread(y), banks(work_bank(a, b)), wide(bo_s[0]), ALU.add))
                    asked[b] = norms.ask(ch, tile(y))
                elif s == 3 and a == 1:
                    ch.link(norms.normalise(dve, ch, asked[b], y, tile(y)))
                    V.tensor_tensor(X[:, b, :], X[:, b, :], y, ALU.add).then_inc(S["x_ready"], 1)
                    dve.wait_ge(S["x_ready"], b + 1)
                    asked[b] = norms.ask(ch, tile(X[:, b, :]))
                elif s == 3:
                    if b < 2:
                        dve.wait_ge(x_loaded[b], 16 if b == 0 else 16 * (B - 1))
                    asked[b] = norms.ask(ch, tile(X[:, b, :]))
                elif s == 4:
                    if a == 0:
                        wait(dve, S["xt_psum"], b - 1)
                    norms.normalise(dve, ch, asked[b], XH[:, b, :] if a else norm[b % 2], tile(X[:, b, :])
                                    ).then_inc(S["xh_ready"], 1)
                elif s == 6:
                    dve.wait_ge(S["v_psum"], b + 1)
                    wait(dve, S["vst_stored"], 16 * UPB * b)
                    for c in range(2):
                        ins = V.tensor_tensor(
                            vsb[:, 4 * c:4 * c + 4, :, 0:HD],
                            PS[:, V_BANK + c, :].rearrange("p (t h d) -> p t h d", t=4, d=HD),
                            bv_s[a][:, :].rearrange("p (a h d) -> p a h d", a=1, d=HD).to_broadcast([P, 4, H, HD]),
                            ALU.add)
                    ins.then_inc(S["v_ready"], 1)
                elif s == 7:
                    dve.wait_ge(S["q_first"], b + 1)
                    V.tensor_tensor(q, q, q0, ALU.subtract).then_inc(S["q_rest"], 1)
                elif s == 8:
                    dve.wait_ge(S["q_second"], b + 1)
                    V.tensor_tensor(q2, q, q1, ALU.subtract).then_inc(S["q_parts"], 1)

            def rest():
                staggered(a, step, BESIDE * a)
                if a == 1:
                    dve.wait_ge(S["xh_ready"], B)

            return step, rest

        def prep_act(act, a):
            S, norms = prep[a], Norms(prep[a])

            def step(b, s):
                w, x, (q, k) = work_bank(a, b), featT[b % 2], (qf[0][b % 2], qf[1][b % 2])
                two, q_two = (PS[:, v:v + 2, :].rearrange("p c n -> p (c n)") for v in (w, 2 * (b % 2)))
                if (b, s) in ((0, 2), (0, 6)):
                    act.wait_ge(weights_loaded[a], LOADED[a])
                if s in (1, 4) or (s == 3 and a == 1):
                    norms.root(act)
                elif s == 2:
                    act.wait_ge(S["ln_psum"], b + 1)
                    nc.scalar.activation(x, two, ACT.Identity, scale=lng_s[:, :], bias=lnb_s[:, :]
                                         ).then_inc(S["lnt_ready"], 1)
                elif s == 5:
                    act.wait_ge(S["xt_psum"], b + 1)
                    nc.scalar.copy(x, two).then_inc(S["xt_ready"], 1)
                elif s == 6:
                    act.wait_ge(S["bqs_ready"], 1)
                    act.wait_ge(S["q_psum"], b + 1)
                    wait(act, S["q_parts"], b - 1)
                    nc.scalar.activation(q, q_two, ACT.Identity, scale=SCALE, bias=bqs_s[a][:, :]
                                         ).then_inc(S["q_taken"], 1)
                    act.wait_ge(S["k_psum"], b + 1)
                    wait(act, S["k_parts"], b - 1)
                    nc.scalar.activation(k, PS[:, K_BANK:K_BANK + 2, :].rearrange("p c n -> p (c n)"),
                                         ACT.Identity, bias=bk_s[a][:, :]).then_inc(S["k_taken"], 1)
                    wait(act, S["qst_stored"][b % 2], 16 * NB * (b // 2))
                    act.wait_ge(S["q_taken"], b + 1)
                    nc.scalar.copy(parts[b % 2][0][0], q).then_inc(S["q_first"], 1)
                    wait(act, S["kst_stored"][b % 2], 16 * NB * (b // 2))
                    act.wait_ge(S["k_taken"], b + 1)
                    nc.scalar.copy(parts[b % 2][1][0], k).then_inc(S["k_first"], 1)
                elif s == 8:
                    act.wait_ge(S["q_rest"], b + 1)
                    nc.scalar.copy(parts[b % 2][0][1], q).then_inc(S["q_second"], 1)
                    act.wait_ge(S["k_rest"], b + 1)
                    nc.scalar.copy(parts[b % 2][1][1], k).then_inc(S["k_second"], 1)

            return step, lambda: staggered(a, step, (BESIDE + 1) * a)

        def prep_pe(pe, a):
            S = prep[a]

            def step(b, s):
                w, x = work_bank(a, b), featT[b % 2]
                if (b, s) in ((0, 2), (0, 5)):
                    pe.wait_ge(weights_loaded[a], LOADED[a])
                if s == 0:
                    pe.wait_ge(S["ol_loaded"], 32 * (b + 1))
                    wait(pe, S["q_taken"], b - 1)
                    wait(pe, S["k_taken"], b - 1)
                    transpose_outputs(w, sum_bank(b)).then_inc(S["ol_psum"], 1)
                elif s == 1:
                    pe.wait_ge(S["ln_ready"], b + 1)
                    transpose_tiles(w, work[b % 2]).then_inc(S["ln_psum"], 1)
                elif s == 2:
                    pe.wait_ge(S["lnt_ready"], b + 1)
                    for t in range(NT):
                        ins = nc.tensor.matmul(PS[:, w + t // 4, (t % 4) * D:(t % 4 + 1) * D],
                                               x[:, t * P:(t + 1) * P], wo_s[0][:, :], start=True, stop=True)
                    ins.then_inc(S["y_psum"], 1)
                elif s == 4:
                    pe.wait_ge(S["xh_ready"], b + 1)
                    wait(pe, S["q_taken"], b - 1)
                    transpose_tiles(w, XH[:, b, :] if a else norm[b % 2]).then_inc(S["xt_psum"], 1)
                elif s == 5:
                    pe.wait_ge(S["xt_ready"], b + 1)
                    wait(pe, S["k_taken"], b)
                    if a == 1:
                        pe.wait_ge(S["o_ready"], min(b + 2, B))
                    for bank, weights, signal in ((2 * (b % 2), wq_s[a], S["q_psum"]), (K_BANK, wk_s[a], S["k_psum"])):
                        for c in range(2):
                            ins = nc.tensor.matmul(PS[:, bank + c, :], weights[:, :], x[:, c * CH:(c + 1) * CH],
                                                   start=True, stop=True)
                        ins.then_inc(signal, 1)
                    wait(pe, S["v_ready"], b)
                    for t in range(NT):
                        ins = nc.tensor.matmul(PS[:, V_BANK + t // 4, (t % 4) * D:(t % 4 + 1) * D],
                                               x[:, t * P:(t + 1) * P], wv_s[a][:, :], start=True, stop=True)
                    ins.then_inc(S["v_psum"], 1)

            def rest():
                staggered(a, step, BESIDE * a)
                for signal in ("q_taken", "k_taken", "v_ready"):
                    pe.wait_ge(S[signal], B)

            return step, rest

        def prep_pool(pool, a):
            S = prep[a]

            def step(b, s):
                k, (k0, k1, k2) = qf[1][b % 2], parts[b % 2][1]
                if s == 7:
                    pool.wait_ge(S["k_first"], b + 1)
                    nc.gpsimd.tensor_tensor(k, k, k0, ALU.subtract).then_inc(S["k_rest"], 1)
                elif s == 8:
                    pool.wait_ge(S["k_second"], b + 1)
                    nc.gpsimd.tensor_tensor(k2, k, k1, ALU.subtract).then_inc(S["k_parts"], 1)

            staggered(a, step)

        def prep_sp(sp, a, early):
            S = prep[a]

            def store(b):
                sp.wait_ge(S["v_ready"], b + 1)
                vals = v_st[a].rearrange("(b u) (t p) w -> b u p t w", u=UPB, p=P)[b]
                for u in range(UPB):
                    sp.dma_start(vals[u], vsb[:, :, HG * u:HG * u + HG, :].rearrange("p t h d -> p t (h d)")
                                 ).then_inc(S["vst_stored"], 16)
                for st, which, pt, signal, ready in (
                        (q_st[a], QPARTS, parts[b % 2][0], S["qst_stored"], S["q_parts"]),
                        (k_st[a], KPARTS, parts[b % 2][1], S["kst_stored"], S["k_parts"])):
                    sp.wait_ge(ready, b + 1)
                    view = st.rearrange("(b u) j c d n -> b c (u j) d n", u=UPB)[b]
                    for c in range(NB):
                        sp.dma_start(view[c], pt[which[c]]).then_inc(signal[b % 2], 16)

            if a == 1:
                for b in range(2, B):
                    sp.wait_ge(S["ol_psum"], b)
                    load_outputs(sp, S["ol_loaded"], 0, b)
            store(0)
            store(1)
            sp.wait_ge(S["qst_stored"][0], 16 * NB)
            sp.wait_ge(S["kst_stored"][0], 16 * NB)
            sp.wait_ge(S["vst_stored"], 16 * UPB)
            early()
            store(2)
            store(3)
            for k in range(2):
                sp.wait_ge(S["qst_stored"][k], 16 * NB * (B // 2))
                sp.wait_ge(S["kst_stored"][k], 16 * NB * (B // 2))
            sp.wait_ge(S["vst_stored"], 16 * UPB * B)

        CHAIN = 4

        def pairwise(eng, body):
            for i in (0,):
                for p in range(2):
                    body(2 * i + p, p, i)
            with eng.Fori(1, UNITS // 2 - 1) as i:
                for p in range(2):
                    body(2 * i + p, p, i)
            for i in (UNITS // 2 - 1,):
                for p in range(2):
                    body(2 * i + p, p, i)

        def ahead(v, p, i, d):
            return v + d, (p + d) % 2, i + (p + d) // 2

        BESIDE_PE = ({0: 0, 3: 1, 5: 2}, {0: 0, 2: 1, 3: 2, 9: 6, 10: 7, 14: 11})
        BESIDE_ACT = ({3: 1, 6: 2, 8: 3, 11: 4}, {3: 1, 7: 4, 10: 6, 12: 8, 15: 11})

        def share(at, u, s, piece):
            if isinstance(u, int) and u == UNITS - 1 and s in at:
                piece(at[s])

        def att_pe(pe, a, beside):
            S, pl = att[a], plans[a]

            def row_scores(v, vp, vi, r):
                qt, half, width, g, hp = pl.rows[r]
                if r == 0:
                    pe.wait_ge(S["row_loaded"][vp], 64 * (vi + 1))
                x = pl.slot_of(r)
                wait(pe, S["row_read"], pl.before(v, x))
                bank = RB + x % RING
                diagonal = pl.causal and qt // 4 == half
                ins = nc.tensor.matmul(PS[:, bank, 0:width], QR[vp][hp][:, g, qt * P:(qt + 1) * P],
                                       KR[vp][:, g, half * CH:half * CH + width],
                                       start=True, stop=not diagonal)
                if diagonal:
                    ins = nc.tensor.matmul(PS[:, bank, width - P:width], identb[:, :], mask_q[:, :],
                                           start=False, stop=True)
                ins.then_inc(S["row_ready"], 1)

            def transpose_maxima(v, vp, stream):
                pe.wait_ge(S["max_ready"], v + 1)
                wait(pe, S["row_read"], pl.before(stream, TSLOT))
                bank = PS[:, RB + TSLOT % RING, :].bitcast(BF16)
                for qt in range(NT):
                    ins = nc.tensor.transpose(bank[0:4 * MROWS, qt * P:(qt + 1) * P],
                                              mparts[vp][:, qt, :, :, :].rearrange("p r m g -> p (r m g)"),
                                              identb[:, :])
                ins.then_inc(S["row_ready"], 1)

            def scores(u, p, i, s, g):
                c, kt = pl.steps[s]
                off = pl.off(c, kt)
                done, signal = (S["exp_a"], S["scores_a"]) if g == 0 else (S["exp_b"], S["scores_b"])
                if s == 0 and g == 0:
                    pe.wait_ge(S["main_loaded"][p], 80 * (i + 1))
                    pe.wait_ge(S["maxrow_loaded"][p], 16 * 2 * (i + 1))
                wait(pe, done, pl.n * u + s)
                diagonal = pl.causal and kt // 4 == c
                for hp in range(2):
                    ins = nc.tensor.matmul(PS[:, TB + 2 * g + hp, off:CH], KS[p][hp][:, g, kt * P:(kt + 1) * P],
                                           QS[p][:, g, c * CH + off:(c + 1) * CH],
                                           start=True, stop=not diagonal)
                if diagonal:
                    for hp in range(2):
                        ins = nc.tensor.matmul(PS[:, TB + 2 * g + hp, off:off + P], identb[:, :],
                                               mask_k[:, :], start=False, stop=True)
                ins.then_inc(signal, 1)

            def values(u, p, s):
                c, kt = pl.steps[s]
                off = pl.off(c, kt)
                pe.wait_ge(S["exp_b"], pl.n * u + s + 1)
                if kt == 0:
                    wait(pe, S["acc_copied"], NC * u + c)
                for h in range(HG):
                    ins = nc.tensor.matmul(PS[32 * h:32 * h + 32, AC, off:CH],
                                           VS[p][:, kt, 9 * h:9 * h + 32], PR[s % PRING][:, h, off:CH],
                                           start=kt == 0, stop=pl.last(s), skip_group_check=True)
                ins.then_inc(S["pv_done"], 1)

            def body(u, p, i):
                for s in range(pl.n):
                    more = pl.stream(u, s)
                    nxt = (u, p, i, s + 1) if s + 1 < pl.n else (*ahead(u, p, i, 1), 0)
                    run_next = not (isinstance(nxt[0], int) and nxt[0] == UNITS)
                    old = (u, p, s - 1) if s else (u - 1, 1 - p, pl.n - 1)
                    run_old = not (isinstance(old[0], int) and old[0] < 0)

                    def maxima(count):
                        for _ in range(count):
                            while more:
                                v, r = more.pop(0)
                                if r is None:
                                    transpose_maxima(v, (p + 1) % 2, v + 1)
                                else:
                                    d = 1 if s + LEAD < pl.n else 2
                                    _, vp, vi = ahead(u, p, i, d)
                                    row_scores(v, vp, vi, r)
                                    break

                    maxima(1)
                    if run_next:
                        scores(*nxt, 0)
                    maxima(1)
                    if run_next:
                        scores(*nxt, 1)
                    maxima(2)
                    if run_old:
                        values(*old)
                    if s == 0 and isinstance(u, int) and u == UNITS - 1:
                        pe.wait_ge(S["row_read"], UNITS * pl.used_slots)
                    share(BESIDE_PE[a], u, s, beside)

            for r in range(pl.nr):
                row_scores(0, 0, 0, r)
            for r in range(TSLOT):
                row_scores(1, 1, 0, r)
            transpose_maxima(0, 0, 1)
            for r in range(TSLOT, TSLOT + MEANWHILE):
                row_scores(1, 1, 0, r)
            scores(0, 0, 0, 0, 0)
            scores(0, 0, 0, 0, 1)
            for r in range(TSLOT + MEANWHILE, 4 * LEAD):
                row_scores(1, 1, 0, r)
            pairwise(pe, body)
            values(UNITS - 1, 1, pl.n - 1)
            pe.wait_ge(S["acc_copied"], NC * UNITS)

        def att_dve(dve, a):
            S, pl = att[a], plans[a]

            def row_max(v, vp, r):
                qt, half, width, g, hp = pl.rows[r]
                x = pl.slot_of(r)
                dve.wait_ge(S["row_ready"], pl.used(v, x))
                nc.vector.tensor_reduce(mx[vp][:, qt, 2 * hp + g, half:half + 1],
                                        PS[:, RB + x % RING, 0:width], AX.X, ALU.max,
                                        negate=True).then_inc(S["row_read"], 1)
                if r == pl.nr - 1:
                    parts_of_max(v, vp)

            def parts_of_max(v, vp):
                dve.wait_ge(S["row_read"], pl.used(v, pl.nr))
                ch = Chain(dve, S["chain"], v * CHAIN)
                m4 = mparts[vp]
                f = nm[:, :].rearrange("p (t r g) -> p t r g", r=2, g=2)
                f2 = nm2[:, :].rearrange("p (t r g) -> p t r g", r=2, g=2)
                ch.link(nc.vector.tensor_reduce(nm[:, :], mx[vp][:, :, :, :].rearrange("p t h k -> p (t h) k"),
                                                AX.X, ALU.min))
                ch.link(nc.vector.tensor_copy(m4[:, :, :, 0, :], f))
                ch.link(nc.vector.tensor_tensor(f2, f, m4[:, :, :, 0, :], ALU.subtract))
                ch.link(nc.vector.tensor_copy(m4[:, :, :, 1, :], f2))
                ins = nc.vector.tensor_tensor(m4[:, :, :, 2, :], f2, m4[:, :, :, 1, :], ALU.subtract)
                ins.then_inc(S["max_ready"], 1)
                dve.wait_ge(S["max_ready"], v + 1)
                assert ch.n == CHAIN

            def rows_of_max(v, vp, i_prev, stream):
                dve.wait_ge(S["row_ready"], pl.used(stream, TSLOT))
                if not (isinstance(v, int) and v < 2):
                    dve.wait_ge(S["maxrow_loaded"][vp], 16 * 2 * i_prev)
                nc.vector.tensor_copy(mrow[vp][:, :],
                                      PS[0:4 * MROWS, RB + TSLOT % RING, :].bitcast(BF16)
                                      ).then_inc(S["row_read"], 1)

            def body(u, p, i):
                for s in range(pl.n):
                    for v, r in pl.stream(u, s):
                        if r is None:
                            _, vp, vi = ahead(u, p, i, 1)
                            rows_of_max(v, vp, vi, v + 1)
                        else:
                            d = 1 if s + LEAD < pl.n else 2
                            row_max(v, (p + d) % 2, r)

            for r in range(pl.nr):
                row_max(0, 0, r)
            for r in range(TSLOT):
                row_max(1, 1, r)
            rows_of_max(0, 0, 0, 1)
            for r in range(TSLOT, 4 * LEAD):
                row_max(1, 1, r)
            pairwise(dve, body)

        def att_act(act, a, beside):
            S, pl = att[a], plans[a]

            def exps(u, s, g):
                c, kt = pl.steps[s]
                off = pl.off(c, kt)
                ready, signal = (S["scores_a"], S["exp_a"]) if g == 0 else (S["scores_b"], S["exp_b"])
                if g == 0:
                    wait(act, S["pv_done"], pl.n * u + s - PRING + 1)
                act.wait_ge(ready, pl.n * u + s + 1)
                nc.scalar.activation(PR[s % PRING][:, 2 * g:2 * g + 2, off:CH],
                                     PS[:, TB + 2 * g:TB + 2 * g + 2, off:CH], ACT.Exp).then_inc(signal, 1)

            def copy_outputs(u, c):
                ends = [s for s in range(pl.n) if pl.last(s)]
                act.wait_ge(S["pv_done"], pl.n * u + ends[c] + 1)
                wait(act, S["o_stored"][c], 64 * u)
                nc.scalar.copy(OS[c][:, :], PS[:, AC, :]).then_inc(S["acc_copied"], 1)

            def body(u, p, i):
                for s in range(pl.n):
                    exps(u, s, 0)
                    exps(u, s, 1)
                    if s == 1 and not (isinstance(u, int) and u == 0):
                        copy_outputs(u - 1, NC - 1)
                    if s > 1 and pl.last(s - 2):
                        copy_outputs(u, pl.steps[s - 2][0])
                    share(BESIDE_ACT[a], u, s, beside)

            pairwise(act, body)
            copy_outputs(UNITS - 1, NC - 1)

        def att_sp(sp, a):
            S, pl = att[a], plans[a]

            def load_stacks(u, q_dst, k_dst, signal):
                for st, dst in ((q_st[a], q_dst), (k_st[a], k_dst)):
                    for hp in range(2):
                        buf = dst[hp] if isinstance(dst, list) else dst
                        sp.dma_start(buf[64 * hp:64 * hp + ROWS, :, :],
                                     st.rearrange("u (g r) c d n -> u r (c d) g n", r=2)[u][hp]
                                     ).then_inc(signal, 16)

            def load_main(u, p):
                load_stacks(u, QS[p], KS[p], S["main_loaded"][p])
                sp.dma_start(VS[p][:, :, 0:VW], v_st[a].rearrange("u (t p) w -> u p t w", p=P)[u]
                             ).then_inc(S["main_loaded"][p], 16)

            def load_row(u, p):
                load_stacks(u, QR[p], KR[p], S["row_loaded"][p])

            def load_maxima(u, p):
                sp.wait_ge(S["row_read"], pl.used(u + 1, TSLOT))
                for hp in range(2):
                    rows = mrow[p][2 * MROWS * hp:2 * MROWS * (hp + 1), :]
                    sp.dma_start(QS[p][64 * hp + ROWS:64 * hp + ROWS + MROWS, :, :], rows
                                 ).then_inc(S["maxrow_loaded"][p], 16)

            def store(u, c):
                sp.wait_ge(S["acc_copied"], NC * u + c + 1)
                for h in range(HG):
                    sp.dma_start(o_st[a][u][h, :, c * CH:(c + 1) * CH], OS[c][32 * h:32 * h + HD + 1, :]
                                 ).then_inc(S["o_stored"][c], 16)

            def load_early(b):
                following = (prep[1], tail)[a]
                for c in range(NC):
                    sp.wait_ge(S["o_stored"][c], 64 * UPB * (b + 1))
                wait(sp, following["ol_psum"], b)
                load_outputs(sp, following["ol_loaded"], a, b)

            def body(u, p, i):
                last = isinstance(u, int) and u + 1 >= UNITS
                if isinstance(u, int) and u == UNITS - 2:
                    load_early(0)
                if not last:
                    sp.wait_ge(S["scores_a"], pl.n * u + 3)
                    load_main(u + 1, 1 - p)
                if not (isinstance(u, int) and u + 2 >= UNITS):
                    sp.wait_ge(S["row_ready"], pl.used(u, pl.nr))
                    load_row(u + 2, p)
                store(u, 0)
                if isinstance(u, int) and u == UNITS - 1:
                    load_early(1)
                if not last:
                    load_maxima(u + 1, 1 - p)
                store(u, 1)

            def first_loads():
                if a == 0:
                    sp.wait_ge(cleared, CLEARED)
                load_row(0, 0)
                load_row(1, 1)
                load_main(0, 0)

            prep_sp(sp, a, first_loads)
            load_maxima(0, 0)
            if a == 0:
                for dst, src in loads[1]:
                    sp.dma_start(dst, src, allow_slow_non_contiguous=True).then_inc(weights_loaded[1], 16)
            pairwise(sp, body)
            for c in range(NC):
                sp.wait_ge(S["o_stored"][c], 64 * UNITS)

        SLOTS = NC * E
        WORK, SMALL = 5, 7
        HALVES = [range(0, NT // 2), range(NT // 2, NT)]
        LATE = {1: 11, 2: 12, 3: 13, 4: 14, 5: 15}
        EARLY = {8: (11,), 9: (12, 13), 10: (14,), 11: (15,)}

        def pieces(eng, b, before, experts, after):
            for n in range(SLOTS):
                experts(n)
                if b + 1 < B:
                    before(b + 1, n)
                if b == B - 1 and n in EARLY:
                    for m in EARLY[n]:
                        after(b, m, HALVES[0])
                if 0 < b < B - 1:
                    after(b - 1, n)
                elif b == B - 1 and n in LATE:
                    after(b - 1, LATE[n])

        def tail_sp(sp):
            S = tail

            def store(b):
                sp.wait_ge(S["out_ready"], b + 1)
                sp.dma_start(out_d.rearrange("b (t p) d -> b p t d", p=P)[b], tiles(res)
                             ).then_inc(S["out_stored"], 16)

            for b in range(2, B):
                sp.wait_ge(S["ol_psum"], b)
                load_outputs(sp, S["ol_loaded"], 1, b)
            for b in range(B - 1):
                store(b)
            for half, tiles_of in enumerate(HALVES):
                sp.wait_ge(S["last_ready"], half + 1)
                of = slice(tiles_of.start, tiles_of.stop)
                sp.dma_start(out_d.rearrange("b (t p) d -> b p t d", p=P)[B - 1][:, of, :], tiles(nat)[:, of, :]
                             ).then_inc(S["last_stored"], 16)
            sp.wait_ge(S["out_stored"], 16 * (B - 1))
            sp.wait_ge(S["last_stored"], 16 * NC)

        def tail_dve(dve):
            S, V = tail, nc.vector
            ch = Chain(dve, S["chain"], 0)
            rows = lambda v: v[:, :].rearrange("p (t a) -> p t a", a=1).to_broadcast([P, NT, E])
            norms = Norms(S)

            def before(b, n):
                x = xf[b % 2]
                if n == 0:
                    dve.wait_ge(S["ol_psum"], b + 1)
                    divide(ch, div[:, :], WORK, SMALL, S["o_ready"])
                elif n == 2:
                    dve.wait_ge(S["y_psum"], b + 1)
                    ch.link(V.tensor_tensor(tiles(x), banks(WORK), wide(bo_s[1]), ALU.add))
                    ch.link(V.tensor_tensor(x[:, :], x[:, :], XH[:, b, :], ALU.add))
                elif n == 3:
                    norms.ask(ch, tile(x))
                elif n == 4:
                    ch.link(norms.normalise(dve, ch, norms.n, x, tile(x)))
                    ch.link(V.tensor_tensor(tiles(x), tiles(x), wide(l1g_s), ALU.mult))
                elif n == 5:
                    V.tensor_tensor(tiles(x), tiles(x), wide(l1b_s), ALU.add).then_inc(S["xf_ready"], 1)
                    dve.wait_ge(S["xf_ready"], b + 1)
                elif n == 7:
                    dve.wait_ge(S["logit_psum"], b + 1)
                    ch.link(V.tensor_tensor(lg[:, :, :], PS[:, SMALL, 0:NT * E].rearrange("p (t e) -> p t e", e=E),
                                            gb_s[:, :].rearrange("p (a e) -> p a e", a=1).to_broadcast([P, NT, E]),
                                            ALU.add))
                    ch.link(V.reduce_max(gs[:, :], lg[:, :, :], AX.X))
                    V.tensor_tensor(lg[:, :, :], lg[:, :, :], rows(gs), ALU.subtract).then_inc(S["shifted"], 1)
                elif n == 8:
                    dve.wait_ge(S["exp_ready"], b + 1)
                    ch.link(V.reduce_sum(gs[:, :], ge[:, :, :], AX.X))
                    ch.link(V.reciprocal(gs[:, :], gs[:, :]))
                    ch.link(V.tensor_tensor(ge[:, :, :], ge[:, :, :], rows(gs), ALU.mult))
                this = ge[:, :, :].rearrange("p t (e a) -> p t e a", a=1).to_broadcast([P, NT, E, E])
                other = ge[:, :, :].rearrange("p t (a e) -> p t a e", a=1).to_broadcast([P, NT, E, E])
                earlier = before_e[:, :, :].rearrange("p (a e) f -> p a e f", a=1).to_broadcast([P, NT, E, E])
                if n == 8:
                    ch.link(V.tensor_tensor(cmp1[:, :, :, :], other, this, ALU.is_gt))
                elif n == 9:
                    ch.link(V.tensor_tensor(cmp2[:, :, :, :], other, this, ALU.is_equal))
                    ch.link(V.tensor_tensor(cmp2[:, :, :, :], cmp2[:, :, :, :], earlier, ALU.mult))
                    ch.link(V.tensor_tensor(cmp1[:, :, :, :], cmp1[:, :, :, :], cmp2[:, :, :, :], ALU.add))
                elif n == 10:
                    ch.link(V.reduce_sum(lg[:, :, :], cmp1[:, :, :, :], AX.X))
                    V.scalar_tensor_tensor(wt[b % 2][:, :, :], lg[:, :, :], 2.0, ge[:, :, :], ALU.is_lt,
                                           ALU.mult).then_inc(S["wt_ready"], 1)
                    dve.wait_ge(S["wt_ready"], b + 1)

            def experts(b):
                def add(n):
                    c, e = n // E, n % E
                    y = acc[b % 2]
                    if e == 0:
                        part = slice(c * CH, (c + 1) * CH)
                        dve.wait_ge(S["bias_psum"], NC * b + c + 1)
                        V.tensor_tensor(y[:, part], xf[b % 2][:, part], PS[:, 4, :], ALU.add
                                        ).then_inc(S["acc_begun"], 1)
                        dve.wait_ge(S["acc_begun"], NC * b + c + 1)
                    else:
                        dve.wait_ge(S["e_added"], SLOTS * b + n)
                    dve.wait_ge(S["e_psum"], SLOTS * b + n + 1)
                    for t in range(4):
                        tt = 4 * c + t
                        yt = y[:, tt * D:(tt + 1) * D]
                        ins = V.scalar_tensor_tensor(yt, PS[:, 2 + n % 2, t * D:(t + 1) * D],
                                                     wt[b % 2][:, tt, e:e + 1], yt, ALU.mult, ALU.add)
                    ins.then_inc(S["e_added"], 1)
                return add

            def after(b, n, tiles=range(NT)):
                y, cols = acc[b % 2], slice(tiles.start * D, tiles.stop * D)
                result, signal = (nat, S["last_ready"]) if b == B - 1 else (res, S["out_ready"])
                count = b + 1 if b < B - 1 else tiles.stop * NC // NT
                if n == 11:
                    dve.wait_ge(S["e_added"], SLOTS * b + E * tiles.stop * NC // NT)
                    norms.ask(ch, tile(y), tiles)
                elif n == 12:
                    ch.link(norms.normalise(dve, ch, norms.n, y, tile(y), tiles))
                elif n == 13:
                    ch.link(V.tensor_tensor(spread(y[:, cols]), spread(y[:, cols]), wide(l2g_s, len(tiles)), ALU.mult))
                    ch.link(V.tensor_tensor(spread(y[:, cols]), spread(y[:, cols]), wide(l2b_s, len(tiles)), ALU.add))
                elif n == 14:
                    norms.ask(ch, tile(y), tiles)
                elif n == 15:
                    ch.link(norms.normalise(dve, ch, norms.n, y, tile(y), tiles))
                    if b < B - 1:
                        wait(dve, S["out_stored"], 16 * b)
                    V.tensor_tensor(result[:, cols], y[:, cols], X[:, b, cols], ALU.add).then_inc(signal, 1)
                    dve.wait_ge(signal, count)

            def run():
                for b in range(B):
                    pieces(dve, b, before, experts(b), after)
                for n in range(SLOTS):
                    after(B - 1, n, HALVES[1])

            return before, run

        def tail_act(act):
            S = tail
            norms = Norms(S)

            def take(dst, src, signal):
                nc.scalar.copy(dst, src).then_inc(signal, 1)

            def before(b, n):
                if n == 1:
                    act.wait_ge(S["on_psum"], b + 1)
                    take(oN[b], PS[:, WORK:WORK + 2, :].rearrange("p c n -> p (c n)"), S["on_ready"])
                elif n == 4:
                    norms.root(act)
                elif n == 6:
                    act.wait_ge(S["xf_psum"], b + 1)
                    take(xTs[b % 2], PS[:, WORK:WORK + 2, :].rearrange("p c n -> p (c n)"), S["xt_ready"])
                elif n == 8:
                    act.wait_ge(S["shifted"], b + 1)
                    nc.scalar.activation(ge[:, :, :], lg[:, :, :], ACT.Exp).then_inc(S["exp_ready"], 1)
                elif n == 11:
                    act.wait_ge(S["wt_psum"], b + 1)
                    take(wT, PS[0:E, WORK:WORK + 2, :].rearrange("p c n -> p (c n)"), S["wT_ready"])

            def relus(m):
                e = m % E
                for f in range(2):
                    act.wait_ge(S["h_psum"], 2 * m + f + 1)
                    nc.scalar.activation(hT[m % 2][:, f, :], PS[:, f, :], ACT.Relu,
                                         bias=b1_s[:, e, f:f + 1]).then_inc(S["h_ready"], 1)

            def experts(b):
                def next_relus(n):
                    if SLOTS * b + n + 1 < SLOTS * B:
                        relus(SLOTS * b + n + 1)
                return next_relus

            def after(b, n, tiles=range(NT)):
                if n in (12, 15):
                    norms.root(act, tiles)

            def run():
                relus(0)
                for b in range(B):
                    pieces(act, b, before, experts(b), after)
                for n in range(SLOTS):
                    after(B - 1, n, HALVES[1])

            return before, run

        def tail_pe(pe):
            S = tail

            def before(b, n):
                if n == 0:
                    pe.wait_ge(S["ol_loaded"], 32 * (b + 1))
                    wait(pe, S["wT_ready"], b)
                    transpose_outputs(WORK, SMALL).then_inc(S["ol_psum"], 1)
                elif n == 1:
                    pe.wait_ge(S["o_ready"], b + 1)
                    transpose_tiles(WORK, div).then_inc(S["on_psum"], 1)
                elif n == 2:
                    pe.wait_ge(S["on_ready"], b + 1)
                    for t in range(NT):
                        ins = nc.tensor.matmul(PS[:, WORK + t // 4, (t % 4) * D:(t % 4 + 1) * D],
                                               oN[b][:, t * P:(t + 1) * P], wo_s[1][:, :], start=True, stop=True)
                    ins.then_inc(S["y_psum"], 1)
                elif n == 6:
                    pe.wait_ge(S["xf_ready"], b + 1)
                    transpose_tiles(WORK, xf[b % 2]).then_inc(S["xf_psum"], 1)
                elif n == 7:
                    pe.wait_ge(S["xt_ready"], b + 1)
                    for t in range(NT):
                        ins = nc.tensor.matmul(PS[:, SMALL, t * E:(t + 1) * E], xTs[b % 2][:, t * P:(t + 1) * P],
                                               gw_s[:, :], start=True, stop=True)
                    ins.then_inc(S["logit_psum"], 1)
                elif n == 11:
                    pe.wait_ge(S["wt_ready"], b + 1)
                    for t in range(NT):
                        ins = nc.tensor.transpose(PS[0:E, WORK + t // 4, (t % 4) * P:(t % 4 + 1) * P],
                                                  wt[b % 2][:, t, :], ident[:, :])
                    ins.then_inc(S["wt_psum"], 1)

            def hidden(m):
                b, c, e = m // SLOTS, m % SLOTS // E, m % E
                if m == 0 or m % SLOTS == 0:
                    pe.wait_ge(S["xt_ready"], b + 1)
                for f in range(2):
                    wait(pe, S["h_ready"], 2 * (m - 1) + f + 1)
                    nc.tensor.matmul(PS[:, f, :], w1_s[:, e, f * P:(f + 1) * P],
                                     xTs[b % 2][:, c * CH:(c + 1) * CH], start=True, stop=True
                                     ).then_inc(S["h_psum"], 1)

            def second(m):
                e = m % E
                pe.wait_ge(S["h_ready"], 2 * m + 2)
                wait(pe, S["e_added"], m - 1)
                for t in range(4):
                    for f in range(2):
                        ins = nc.tensor.matmul(PS[:, 2 + m % 2, t * D:(t + 1) * D],
                                               hT[m % 2][:, f, t * P:(t + 1) * P], w2_s[:, e, f, :],
                                               start=f == 0, stop=f == 1)
                ins.then_inc(S["e_psum"], 1)

            def bias(b, c):
                pe.wait_ge(S["wT_ready"], b + 1)
                wait(pe, S["acc_begun"], NC * b + c)
                for t in range(4):
                    tt = 4 * c + t
                    ins = nc.tensor.matmul(PS[:, 4, t * D:(t + 1) * D], wT[:, tt * P:(tt + 1) * P],
                                           b2_s[:, :], start=True, stop=True)
                ins.then_inc(S["bias_psum"], 1)

            def experts(b):
                def expert(n):
                    m = SLOTS * b + n
                    if n % E == 0:
                        bias(b, n // E)
                    if m + 1 < SLOTS * B:
                        hidden(m + 1)
                    second(m)
                return expert

            def run():
                hidden(0)
                for b in range(B):
                    pieces(pe, b, before, experts(b), lambda b, n, tiles=None: None)

            return before, run

        @block.sync
        def _(sp):
            sp.dma_start(spread(X[:, 0, :]), x_view[0]).then_inc(x_loaded[0], 16)
            for dst, src in loads[0]:
                sp.dma_start(dst, src, allow_slow_non_contiguous=True).then_inc(weights_loaded[0], 16)
            for b in range(1, B):
                sp.dma_start(spread(X[:, b, :]), x_view[b]).then_inc(x_loaded[1], 16)
            att_sp(sp, 0)
            att_sp(sp, 1)
            tail_sp(sp)

        @block.vector
        def _(dve):
            for p in range(2):
                nc.vector.memset(mx[p][:, :, :, :], 3e38)
            nc.vector.memset(before_e[:, :, :], 0.0).then_inc(const_dve, 1)
            dve.wait_ge(const_dve, 1)
            for e in range(1, E):
                ins = nc.vector.memset(before_e[:, e, 0:e], 1.0)
            ins.then_inc(const_dve, 1)
            dve.wait_ge(const_dve, 2)
            _, prepare = prep_dve(dve, 0)
            prepare()
            att_dve(dve, 0)
            step, prepare = prep_dve(dve, 1)
            for n in range(BESIDE):
                step(0, n)
            prepare()
            att_dve(dve, 1)
            before, experts = tail_dve(dve)
            for n in range(SLOTS):
                before(0, n)
            experts()

        @block.scalar
        def _(act):
            _, prepare = prep_act(act, 0)
            prepare()
            step, prepare = prep_act(act, 1)
            att_act(act, 0, lambda n: step(0, n))
            step(0, BESIDE)
            prepare()
            before, experts = tail_act(act)
            att_act(act, 1, lambda n: before(0, n))
            experts()

        @block.gpsimd
        def _(pool):
            nc.gpsimd.memset(ident[:, :], 0.0)
            nc.gpsimd.memset(mask_q[:, :], 0.0)
            nc.gpsimd.memset(mask_k[:, :], 0.0).then_inc(const_ready, 1)
            pool.wait_ge(const_ready, 1)
            nc.gpsimd.affine_select(out=ident[:, :], in_=ident[:, :], compare_op=ALU.not_equal, fill=1.0,
                                    base=0, pattern=[[-1, P]], channel_multiplier=1)
            nc.gpsimd.affine_select(out=mask_q[:, :], in_=mask_q[:, :], compare_op=ALU.is_ge, fill=NEG,
                                    base=0, pattern=[[-1, P]], channel_multiplier=1)
            nc.gpsimd.affine_select(out=mask_k[:, :], in_=mask_k[:, :], compare_op=ALU.is_ge, fill=NEG,
                                    base=0, pattern=[[1, P]], channel_multiplier=-1).then_inc(const_ready, 1)
            pool.wait_ge(const_ready, 2)
            nc.gpsimd.tensor_copy(identb[:, :], ident[:, :]).then_inc(const_ready, 1)
            nc.gpsimd.memset(vsb[:, :, :, :], 1.0).then_inc(cleared, 1)
            for buf in (*KS[0], *KS[1], *QR[0], *QR[1], *QS, *KR, *VS):
                ins = nc.gpsimd.memset(buf[:, :, :], 0.0)
            for h in range(2):
                ins.then_inc(cleared, 1)
                pool.wait_ge(cleared, h + 2)
                for p in range(2):
                    ins = nc.gpsimd.memset(KS[p][h][64 * h:64 * h + 64, :, :], 1.0)
            ins.then_inc(cleared, 1)
            pool.wait_ge(cleared, CLEARED)
            prep_pool(pool, 0)
            prep_pool(pool, 1)

        @block.tensor
        def _(pe):
            pe.wait_ge(const_ready, 3)
            _, prepare = prep_pe(pe, 0)
            prepare()
            step, prepare = prep_pe(pe, 1)
            att_pe(pe, 0, lambda n: step(0, n))
            step(0, BESIDE - 1)
            prepare()
            before, experts = tail_pe(pe)
            att_pe(pe, 1, lambda n: before(0, n))
            experts()


_INS = ["L0_attn_x"] + ["L0_attn_" + n for n in "Wq bq Wk bk Wv bv ln_g ln_b Wo bo".split()] + \
       ["L0_ffn_" + n for n in "Wq bq Wk bk Wv bv Wo bo gW gb W1 b1 W2 b2 ln1_g ln1_b ln2_g ln2_b".split()]


def kernel(**inputs):
    import numpy as _np
    import concourse.bacc as _bacc
    from concourse import mybir as _mybir
    from concourse.bass_utils import run_bass_kernel_spmd as _run

    nc = _bacc.Bacc("TRN2", target_bir_lowering=False, num_devices=1)
    arrays, args = {}, []
    for name in _INS:
        a = _np.ascontiguousarray(inputs[name])
        arrays[f"in_{name}_dram"] = a
        args.append(nc.dram_tensor(f"in_{name}_dram", a.shape, _mybir.dt.from_np(a.dtype), kind="ExternalInput").ap())
    args.append(nc.dram_tensor("out_0_dram", (B, N, D), _mybir.dt.float32, kind="ExternalOutput").ap())
    sandwich(nc, *args)
    r = _run(nc, [arrays], core_ids=[0])
    return r.results[0]["out_0_dram"]
```
